# Optimizing a Trainium2 kernel written in Bass

```python
import numpy as np
import jax
import jax.numpy as jnp

def _softmax(x, axis=-1):
    return jax.nn.softmax(x, axis=axis)

def _gelu(x):
    return jax.nn.gelu(x, approximate=True)

def _silu(x):
    return jax.nn.silu(x)

def _sigmoid(x):
    return jax.nn.sigmoid(x)

def _layernorm(x, axis=-1, eps=1e-05):
    m = jnp.mean(x, axis=axis, keepdims=True)
    v = jnp.var(x, axis=axis, keepdims=True)
    return (x - m) / jnp.sqrt(v + eps)

def _scatter_add(tgt, idx, src, axis=0):
    return tgt.at[idx].add(src)

def _segment_sum(src, seg, n):
    return jax.ops.segment_sum(src, seg, n)
kernel_name = 'mk_seq_preln_d2_jaxref_r8_2ea513'

def setup_inputs(seed: int=0):
    np.random.seed(seed)
    _w = jnp.asarray

    def _L0_attn_setup():
        import jax, jax.numpy as jnp
        import numpy as np
        D_MODEL = 128
        B, S = (4, 512)

        def _linear_scan(x_scan, a):

            def combine(l, r):
                al, xl = l
                ar, xr = r
                return (al * ar, ar * xl + xr)
            _, h = jax.lax.associative_scan(combine, (a, x_scan), axis=1)
            return h
        key = jax.random.key(seed)
        ks = jax.random.split(key, 4)
        scale = 1.0 / np.sqrt(D_MODEL)
        return {'x': jax.random.normal(ks[0], (B, S, D_MODEL), dtype=jnp.float32), 'Wg': jax.random.normal(ks[1], (D_MODEL, D_MODEL), dtype=jnp.float32) * scale, 'bg': jnp.zeros((D_MODEL,), dtype=jnp.float32), 'Wv': jax.random.normal(ks[2], (D_MODEL, D_MODEL), dtype=jnp.float32) * scale, 'bv': jnp.zeros((D_MODEL,), dtype=jnp.float32), 'Wd': jax.random.normal(ks[3], (D_MODEL, D_MODEL), dtype=jnp.float32) * scale, 'bd': jnp.ones((D_MODEL,), dtype=jnp.float32)}
    _L0_attn_in = _L0_attn_setup()

    def _L0_ffn_setup():
        import jax, jax.numpy as jnp
        import numpy as np
        DIM = 128
        HIDDEN = 256
        N_EXPERTS = 8
        TOP_K = 2
        EPS = 1e-06

        def rms_norm(x, scale, eps=EPS):
            ms = jnp.mean(jnp.square(x.astype(jnp.float32)), axis=-1, keepdims=True)
            s = scale.astype(jnp.float32) * jax.lax.rsqrt(ms + eps)
            return x * s.astype(x.dtype)

        def moe_linear(xf, ids, W):
            E = W.shape[0]
            out = jnp.zeros((xf.shape[0], W.shape[1]), dtype=xf.dtype)
            for e in range(E):
                out = out + jnp.where((ids == e)[:, None], xf @ W[e].T, 0.0)
            return out
        key = jax.random.key(seed)
        k1, k2, k3, k4 = jax.random.split(key, 4)
        x = jax.random.normal(k1, (4, 512, DIM), dtype=jnp.float32)
        norm_scale = jnp.ones((DIM,), dtype=jnp.float32)
        w_router = jax.random.normal(k2, (N_EXPERTS, DIM), dtype=jnp.float32) / np.sqrt(DIM)
        lim_up = np.sqrt(6.0 / (DIM + 2 * HIDDEN))
        w_up = jax.random.uniform(k3, (N_EXPERTS, 2 * HIDDEN, DIM), dtype=jnp.float32, minval=-lim_up, maxval=lim_up)
        lim_dn = np.sqrt(6.0 / (HIDDEN + DIM))
        w_down = jax.random.uniform(k4, (N_EXPERTS, DIM, HIDDEN), dtype=jnp.float32, minval=-lim_dn, maxval=lim_dn)
        return {'x': x, 'norm_scale': norm_scale, 'w_router': w_router, 'w_up': w_up, 'w_down': w_down}
    _L0_ffn_in = _L0_ffn_setup()

    def _L1_attn_setup():
        import jax, jax.numpy as jnp
        import numpy as np
        H = 8
        D = 64
        E = 128

        def sinusoidal_pe(T, d, dtype=jnp.float32):
            pos = jnp.arange(T, dtype=jnp.float32)[:, None]
            div = jnp.exp(jnp.arange(0, d, 2, dtype=jnp.float32) * (-np.log(10000.0) / d))
            ang = pos * div
            pe = jnp.stack([jnp.sin(ang), jnp.cos(ang)], axis=-1).reshape(T, d)
            return pe.astype(dtype)
        key = jax.random.key(seed)
        k1, k2, k3 = jax.random.split(key, 3)
        B, T = (2, 256)
        x = jax.random.normal(k1, (B, T, E), dtype=jnp.float32)
        Wqkv = jax.random.normal(k2, (3 * H * D, E), dtype=jnp.float32) * (1.0 / np.sqrt(E))
        Wo = jax.random.normal(k3, (E, H * D), dtype=jnp.float32) * (1.0 / np.sqrt(H * D))
        return {'x': x, 'Wqkv': Wqkv, 'Wo': Wo}
    _L1_attn_in = _L1_attn_setup()

    def _L1_ffn_setup():
        import jax, jax.numpy as jnp
        import numpy as np
        D_MODEL = 128
        D_FF = 512
        NUM_EXPERTS = 8
        B, N = (16, 128)
        key = jax.random.key(seed)
        ks = jax.random.split(key, 7)
        s_in = 1.0 / np.sqrt(D_MODEL)
        s_ff = 1.0 / np.sqrt(D_FF)
        return {'x': jax.random.normal(ks[0], (B, N, D_MODEL), dtype=jnp.float32), 'Wr': jax.random.uniform(ks[1], (D_MODEL, NUM_EXPERTS), jnp.float32, -s_in, s_in), 'br': jax.random.uniform(ks[2], (NUM_EXPERTS,), jnp.float32, -s_in, s_in), 'W1': jax.random.uniform(ks[3], (NUM_EXPERTS, D_MODEL, D_FF), jnp.float32, -s_in, s_in), 'b1': jax.random.uniform(ks[4], (NUM_EXPERTS, D_FF), jnp.float32, -s_in, s_in), 'W2': jax.random.uniform(ks[5], (NUM_EXPERTS, D_FF, D_MODEL), jnp.float32, -s_ff, s_ff), 'b2': jax.random.uniform(ks[6], (NUM_EXPERTS, D_MODEL), jnp.float32, -s_ff, s_ff)}
    _L1_ffn_in = _L1_ffn_setup()
    _d = {'L0_attn_x': _L0_attn_in['x'], 'L0_attn_Wg': _L0_attn_in['Wg'], 'L0_attn_bg': _L0_attn_in['bg'], 'L0_attn_Wv': _L0_attn_in['Wv'], 'L0_attn_bv': _L0_attn_in['bv'], 'L0_attn_Wd': _L0_attn_in['Wd'], 'L0_attn_bd': _L0_attn_in['bd'], 'L0_ffn_norm_scale': _L0_ffn_in['norm_scale'], 'L0_ffn_w_router': _L0_ffn_in['w_router'], 'L0_ffn_w_up': _L0_ffn_in['w_up'], 'L0_ffn_w_down': _L0_ffn_in['w_down'], 'L1_attn_Wqkv': _L1_attn_in['Wqkv'], 'L1_attn_Wo': _L1_attn_in['Wo'], 'L1_ffn_Wr': _L1_ffn_in['Wr'], 'L1_ffn_br': _L1_ffn_in['br'], 'L1_ffn_W1': _L1_ffn_in['W1'], 'L1_ffn_b1': _L1_ffn_in['b1'], 'L1_ffn_W2': _L1_ffn_in['W2'], 'L1_ffn_b2': _L1_ffn_in['b2']}
    _x0 = _d['L0_attn_x']
    _d['L0_attn_x'] = jax.random.normal(jax.random.fold_in(jax.random.key(seed), 1), (2, 1024, 128), dtype=_x0.dtype)
    del _x0
    return _d

def reference(L0_attn_x, L0_attn_Wg, L0_attn_bg, L0_attn_Wv, L0_attn_bv, L0_attn_Wd, L0_attn_bd, L0_ffn_norm_scale, L0_ffn_w_router, L0_ffn_w_up, L0_ffn_w_down, L1_attn_Wqkv, L1_attn_Wo, L1_ffn_Wr, L1_ffn_br, L1_ffn_W1, L1_ffn_b1, L1_ffn_W2, L1_ffn_b2):

    def _L0_attn_ref(x, Wg, bg, Wv, bv, Wd, bd):
        import jax, jax.numpy as jnp
        import numpy as np
        D_MODEL = 128
        B, S = (4, 512)

        def _linear_scan(x_scan, a):

            def combine(l, r):
                al, xl = l
                ar, xr = r
                return (al * ar, ar * xl + xr)
            _, h = jax.lax.associative_scan(combine, (a, x_scan), axis=1)
            return h
        g = jnp.einsum('bsd,de->bse', x, Wg) + bg
        v = jnp.einsum('bsd,de->bse', x, Wv) + bv
        d = jnp.einsum('bsd,de->bse', x, Wd) + bd
        x_scan = jax.nn.sigmoid(g) * jnp.tanh(v)
        a = 0.001 + 0.998 * jax.nn.sigmoid(d)
        return _linear_scan(x_scan, a)

    def _L0_ffn_ref(x, norm_scale, w_router, w_up, w_down):
        import jax, jax.numpy as jnp
        import numpy as np
        DIM = 128
        HIDDEN = 256
        N_EXPERTS = 8
        TOP_K = 2
        EPS = 1e-06

        def rms_norm(x, scale, eps=EPS):
            ms = jnp.mean(jnp.square(x.astype(jnp.float32)), axis=-1, keepdims=True)
            s = scale.astype(jnp.float32) * jax.lax.rsqrt(ms + eps)
            return x * s.astype(x.dtype)

        def moe_linear(xf, ids, W):
            E = W.shape[0]
            out = jnp.zeros((xf.shape[0], W.shape[1]), dtype=xf.dtype)
            for e in range(E):
                out = out + jnp.where((ids == e)[:, None], xf @ W[e].T, 0.0)
            return out
        B, S, D = x.shape
        skip = x
        xn = rms_norm(x, norm_scale)
        scores = (xn @ w_router.T).astype(jnp.float32)
        scores_topk, idx = jax.lax.top_k(scores, TOP_K)
        weights = jax.nn.softmax(scores_topk, axis=-1)
        xf = jnp.broadcast_to(xn[..., None, :], (B, S, TOP_K, D)).reshape(-1, D)
        ids = idx.reshape(-1)
        up = moe_linear(xf, ids, w_up)
        u, gate = jnp.split(up, 2, axis=-1)
        h = u * jax.nn.silu(gate)
        down = moe_linear(h, ids, w_down)
        down = down.reshape(B, S, TOP_K, D)
        out = jnp.sum(down * weights[..., None].astype(down.dtype), axis=-2)
        return out + skip

    def _L1_attn_ref(x, Wqkv, Wo):
        import jax, jax.numpy as jnp
        import numpy as np
        H = 8
        D = 64
        E = 128

        def sinusoidal_pe(T, d, dtype=jnp.float32):
            pos = jnp.arange(T, dtype=jnp.float32)[:, None]
            div = jnp.exp(jnp.arange(0, d, 2, dtype=jnp.float32) * (-np.log(10000.0) / d))
            ang = pos * div
            pe = jnp.stack([jnp.sin(ang), jnp.cos(ang)], axis=-1).reshape(T, d)
            return pe.astype(dtype)
        B, T, _ = x.shape
        qkv = jnp.einsum('bte,fe->btf', x, Wqkv)
        qkv = qkv.reshape(B, T, H, 3 * D)
        q, k, v = jnp.split(qkv, 3, axis=-1)
        q = q.transpose(0, 2, 1, 3)
        k = k.transpose(0, 2, 1, 3)
        v = v.transpose(0, 2, 1, 3)
        pe = sinusoidal_pe(T, D, q.dtype)
        q = q + pe[None, None]
        k = k + pe[None, None]
        causal = jnp.tril(jnp.ones((T, T), dtype=bool))
        scores = jnp.einsum('bhtd,bhsd->bhts', q, k) / jnp.sqrt(jnp.asarray(D, q.dtype))
        scores = jnp.where(causal[None, None], scores, jnp.asarray(-jnp.inf, q.dtype))
        probs = jax.nn.softmax(scores, axis=-1)
        attn = jnp.einsum('bhts,bhsd->bhtd', probs, v)
        out = attn.transpose(0, 2, 1, 3).reshape(B, T, H * D)
        out = jnp.einsum('btf,ef->bte', out, Wo)
        return out

    def _L1_ffn_ref(x, Wr, br, W1, b1, W2, b2):
        import jax, jax.numpy as jnp
        import numpy as np
        D_MODEL = 128
        D_FF = 512
        NUM_EXPERTS = 8
        B, N = (16, 128)
        scores = jnp.einsum('bh,he->be', x.mean(axis=1), Wr) + br
        top1 = jnp.argmax(scores, axis=-1)
        w1 = W1[top1]
        c1 = b1[top1]
        w2 = W2[top1]
        c2 = b2[top1]
        h = jax.nn.relu(jnp.einsum('bnh,bhf->bnf', x, w1) + c1[:, None, :])
        out = jnp.einsum('bnf,bfh->bnh', h, w2) + c2[:, None, :]
        return out
    x = L0_attn_x
    x = x + _L0_attn_ref(_layernorm(x, axis=-1), L0_attn_Wg, L0_attn_bg, L0_attn_Wv, L0_attn_bv, L0_attn_Wd, L0_attn_bd)
    x = x + _L0_ffn_ref(_layernorm(x, axis=-1), L0_ffn_norm_scale, L0_ffn_w_router, L0_ffn_w_up, L0_ffn_w_down)
    x = x + _L1_attn_ref(_layernorm(x, axis=-1), L1_attn_Wqkv, L1_attn_Wo)
    x = x + _L1_ffn_ref(_layernorm(x, axis=-1), L1_ffn_Wr, L1_ffn_br, L1_ffn_W1, L1_ffn_b1, L1_ffn_W2, L1_ffn_b2)
    return x

_drawn_inputs = setup_inputs


def setup_inputs(seed=0):
    import zlib

    import numpy as np

    out = dict(_drawn_inputs(seed))
    spreads = {'L0_attn_bg': (0.0, 0.421),
     'L0_attn_bv': (0.0, 0.1),
     'L0_attn_bd': (1.0, 0.2),
     'L0_ffn_norm_scale': (1.0, 0.2)}
    factors = {'L1_ffn_b1': 6.125, 'L1_ffn_b2': 4.911}
    for name, (base, spread) in spreads.items():
        noise = np.random.default_rng([zlib.crc32(name.encode()), seed]).standard_normal(out[name].shape)
        drawn = base * np.exp(spread * noise) if base else spread * noise
        out[name] = jnp.asarray(drawn.astype(out[name].dtype))
    for name, factor in factors.items():
        out[name] = (out[name] * factor).astype(out[name].dtype)
    return out
```

```python
from contextlib import ExitStack

import concourse.bass as bass
from concourse import mybir

F32 = mybir.dt.float32
F32R = mybir.dt.float32r
BF16 = mybir.dt.bfloat16
U32 = mybir.dt.uint32
ALU = mybir.AluOpType
ACT = mybir.ActivationFunctionType
AX_X = mybir.AxisListType.X

P = 128
D = 128
B, T = 2, 1024
NT = B * T // P
TB = T // P
G = 512
NG = B * T // G
GB = T // G
TG = G // P
EPS_LN, EPS_RMS = 1e-5, 1e-6
NE, HID = 8, 256
HC = HID // P
NH, HD = 8, 64
NP = B * NH // 2
NHD = B * NH
FF = 512
FC = FF // P
PT_RING = 3

STEPS = [(g, j, max(G * g, P * j), G * (g + 1) - max(G * g, P * j)) for g in range(GB) for j in range(TG * (g + 1))]
NS = len(STEPS)
CHUNKS = [(i, c, min(G, P * (i + 1) - G * c)) for i in range(TB) for c in range(i // TG + 1)]
NC = len(CHUNKS)
MAX_AT = [[0], [1], [2], [3], [4, 5], [6, 7], [8, 9], [10, 11], [], [], [], []]
PROJ_AT = {0: 0, 2: 1, 4: 2, 6: 3}


def mixed_layers_kernel(nc, x, wg, wv0, wd, gate_bias, ns, wr0, wexp, wqk, wv, wo, wr1, br1, wffn, b2,
                        ident_d, mask_d, maskt_d, pe_d, iota_d, out):
    with ExitStack() as ctx:
        def sb(name, shape, dt=F32):
            return ctx.enter_context(nc.sbuf_tensor(name, shape, dt))

        def pb(name):
            return ctx.enter_context(nc.psum_tensor(name, [P, G], F32))

        def sem(name):
            return ctx.enter_context(nc.semaphore(name))

        xres = sb("xres", [P, NT, D])
        xn = sb("xn", [P, NT, D])
        xrms = sb("xrms", [P, NT, D])
        xT = sb("xT", [P, B * T])
        stats = sb("stats", [P, NT, 6])
        mv = sb("mv", [P, NT, 2])
        rstd = sb("rstd", [P, NT])
        rtmp = sb("rtmp", [P, 4, NT])
        rrms = sb("rrms", [P, NT])
        mhalf = sb("mhalf", [P, NT])
        ident = sb("ident", [P, P])
        identb = sb("identb", [P, P], BF16)
        mask = sb("mask", [P, P])
        maskt = sb("maskt", [P, P])
        maskb = sb("maskb", [P, P], BF16)
        masktb = sb("masktb", [P, P], BF16)
        pe = sb("pe", [P, T])
        iota = sb("iota", [P, NE])
        ones = sb("ones", [P, P])
        w_rec = sb("w_rec", [P, 3, D])
        rec_bias = sb("rec_bias", [P, 3])
        ns_sb = sb("ns_sb", [P, 1])
        wr0_sb = sb("wr0_sb", [P, NE])
        wexp_sb = sb("wexp_sb", [P, 2, 2 * HID + HC * D])
        wqk_sb = sb("wqk_sb", [P, NH // 2, 2 * P])
        wv_sb = sb("wv_sb", [P, NH * HD])
        wo_sb = sb("wo_sb", [P, FC, D])
        wr1_sb = sb("wr1_sb", [P, NE])
        br1_sb = sb("br1_sb", [1, NE])
        wffn_sb = sb("wffn_sb", [P, B, FF + FC * D + FC])
        b2_sb = sb("b2_sb", [1, B, D])
        scores = sb("scores", [P, NT, NE])
        top = sb("top", [P, NT, 8])
        topi = sb("topi", [P, NT, 8], U32)
        topf = sb("topf", [P, NT, 2])
        gap = sb("gap", [P, NT])
        egap = sb("egap", [P, NT])
        prob = sb("prob", [P, 2, NT])
        chosen = sb("chosen", [P, 2, NT, NE])
        cw = sb("cw", [P, NT, NE])
        vals = sb("vals", [P, NT, NH, HD + 1])
        qk = sb("qk", [P, 2, 2, 2, T])
        qkr = sb("qkr", [P, 2, 2, T], F32R)
        pt = sb("pt", [P, PT_RING, G])
        att = sb("att", [P, NT, NH * HD])
        mx = sb("mx", [P, 2, TB, 2])
        mfin = sb("mfin", [P, 2, TB])
        nmt = sb("nmt", [TB, 2, P])
        rden = sb("rden", [P, 2, TG])
        attT = sb("attT", [P, 2, FC, P])
        mean_sb = sb("mean_sb", [P, B])
        sc1 = sb("sc1", [1, B, NE])
        top1 = sb("top1", [1, B, 8])
        top1i = sb("top1i", [1, B, 8], U32)

        early = att[:].rearrange("p t f -> p (t f)")
        sig = early[:, 0:2 * G].rearrange("p (a n) -> p a n", a=2)
        tnh = early[:, 2 * G:4 * G].rearrange("p (a n) -> p a n", a=2)
        dec = early[:, 4 * G:6 * G].rearrange("p (a n) -> p a n", a=2)
        scan_in = early[:, 6 * G:8 * G].rearrange("p (a n) -> p a n", a=2)
        hT = early[:, 8 * G:12 * G]
        flat = qk[:].rearrange("p a b c n -> p (a b c n)")
        silu = flat[:, 0:2 * G].rearrange("p (a n) -> p a n", a=2)
        hid = flat[:, 2 * G:6 * G].rearrange("p (a n) -> p a n", a=4)
        hid2 = flat[:, 8 * G:16 * G].rearrange("p (a c n) -> p a c n", a=2, c=FC)

        bank = [pb(f"bank{i}") for i in range(8)]

        ld_x, ld_w = [sem("ld_x0"), sem("ld_x1")], sem("ld_w")
        ld_exp = [sem("ld_exp0"), sem("ld_exp1")]
        ld_ffn = [sem("ld_ffn0"), sem("ld_ffn1")]
        consts, narrowed = sem("consts"), sem("narrowed")
        bn = [sem(f"bn{s}") for s in range(4)]
        mvr = [sem(f"mv{s}") for s in range(4)]
        ve = [sem(f"ve{s}") for s in range(4)]
        rs = [sem(f"rstd{s}") for s in range(4)]
        xnr = [sem(f"xn{s}") for s in range(4)]
        tr = [sem(f"tr{s}") for s in range(4)]
        xtr = [sem(f"xt{s}") for s in range(4)]
        proj0, gates = sem("proj0"), sem("gates")
        dvs, krow = sem("dvs"), sem("krow")
        scanned, back, res1 = sem("scanned"), sem("back"), sem("res1")
        rms = sem("rms")
        rout, gapr, egr, cwr = sem("rout"), sem("gapr"), sem("egr"), sem("cwr")
        up, si, hd, dn, cmb = sem("up"), sem("si"), sem("hd"), sem("dn"), sem("cmb")
        vp, vr = sem("vp"), sem("vr")
        pj, qkd, hi = sem("pj"), sem("qkd"), sem("hi")
        mp, mr, mf, mt, nm, mrow = sem("mp"), sem("mr"), sem("mf"), sem("mt"), sem("nm"), sem("mrow")
        st, ex, pv, den, on = sem("st"), sem("ex"), sem("pv"), sem("den"), sem("on")
        ot, otr, yo, res3 = sem("ot"), sem("otr"), sem("yo"), sem("res3")
        mn, mnr, sc, idx = sem("mn"), sem("mnr"), sem("sc"), sem("idx")
        h2, h2r, y2, res4, stored = sem("h2"), sem("h2r"), sem("y2"), sem("res4"), sem("stored")

        x_v = x.rearrange("(t p) d -> p t d", p=P)
        out_v = out.rearrange("(t p) d -> p t d", p=P)
        loads = [(w_rec[:, 0, :], wg), (w_rec[:, 1, :], wv0), (w_rec[:, 2, :], wd), (rec_bias[:], gate_bias),
                 (ident[:], ident_d), (ns_sb[:], ns), (wr0_sb[:], wr0), (iota[:], iota_d),
                 (mask[:], mask_d), (maskt[:], maskt_d), (pe[:], pe_d),
                 (wqk_sb[:], wqk), (wv_sb[:], wv), (wo_sb[:], wo), (wr1_sb[:], wr1), (br1_sb[:], br1)]
        ALL_W = 16 * len(loads)

        block = ctx.enter_context(nc.Block())

        @block.sync
        def _(sp):
            for g in range(NG):
                sp.dma_start(xres[:, TG * g:TG * (g + 1), :], x_v[:, TG * g:TG * (g + 1), :]).then_inc(ld_x[g // GB], 16)
            for e in range(NE):
                if e >= 2:
                    sp.wait_ge(dn, (e - 1) * NG)
                sp.dma_start(wexp_sb[:, e % 2, :], wexp[e]).then_inc(ld_exp[e % 2], 16)
            for n in range(NHD):
                sp.wait_ge(nm, n + 1)
                a, pr = n % 2, n // 2
                sp.dma_start(qk[HD:HD + 1, pr % 2, a, 0, :], nmt[:, a, :]).then_inc(mrow, 16)
            for b in range(B):
                sp.wait_ge(idx, 2 * (b + 1))
                e = sp.value_load(top1i[0:1, b, 0:1], min_val=0, max_val=NE - 1)
                sp.dma_start(wffn_sb[:, b, :], wffn[bass.ds(e, 1)].rearrange("a p n -> (a p) n")).then_inc(ld_ffn[b], 16)
                sp.dma_start(b2_sb[:, b, :], b2[bass.ds(e, 1), :]).then_inc(ld_ffn[b], 16)
            for g in range(NG):
                sp.wait_ge(res4, g + 1)
                sp.dma_start(out_v[:, TG * g:TG * (g + 1), :], xres[:, TG * g:TG * (g + 1), :]).then_inc(stored, 16)
            sp.wait_ge(stored, 16 * NG)

        @block.gpsimd
        def _(pool):
            nc.gpsimd.memset(mhalf[:], -0.5).then_inc(consts, 1)
            nc.gpsimd.memset(ones[:], 1.0).then_inc(consts, 1)
            nc.gpsimd.memset(vals[:, :, :, HD:HD + 1], 1.0).then_inc(consts, 1)
            nc.gpsimd.memset(mx[:], -3.0e38).then_inc(consts, 1)
            pool.wait_ge(consts, 4)
            for s in range(4):
                if s == 2:
                    pool.wait_ge(cmb, NE * NG)
                    for i in range(4):
                        nc.gpsimd.memset(qk[HD:HD + 1, i // 2, i % 2, 1, :], 1.0).then_inc(krow, 1)
                        pool.wait_ge(krow, i + 1)
                for b in range(B):
                    t = slice(TB * b, TB * (b + 1))
                    k = 6 * b if s == 1 else 2 * b
                    pool.wait_ge(mvr[s], TB * (b + 1))
                    nc.gpsimd.tensor_scalar_add(rtmp[:, 0, t], mv[:, t, 1], EPS_LN).then_inc(ve[s], 1)
                    pool.wait_ge(ve[s], k + 1)
                    nc.gpsimd.tensor_tensor(rstd[:, t], rtmp[:, 0, t], mhalf[:, t], ALU.pow).then_inc(rs[s], 1)
                    if s != 1:
                        pool.wait_ge(rs[s], b + 1)
                        nc.gpsimd.tensor_copy(rtmp[:, 1, t], rstd[:, t]).then_inc(ve[s], 1)
                        continue
                    pool.wait_ge(rs[1], b + 1)
                    nc.gpsimd.tensor_tensor(rtmp[:, 1, t], rstd[:, t], rstd[:, t], ALU.mult).then_inc(ve[s], 1)
                    pool.wait_ge(ve[s], k + 2)
                    nc.gpsimd.tensor_tensor(rtmp[:, 2, t], rtmp[:, 1, t], mv[:, t, 1], ALU.mult).then_inc(ve[s], 1)
                    pool.wait_ge(ve[s], k + 3)
                    nc.gpsimd.tensor_scalar_add(rtmp[:, 3, t], rtmp[:, 2, t], EPS_RMS).then_inc(ve[s], 1)
                    pool.wait_ge(ve[s], k + 4)
                    nc.gpsimd.tensor_tensor(rtmp[:, 1, t], rtmp[:, 3, t], mhalf[:, t], ALU.pow).then_inc(ve[s], 1)
                    pool.wait_ge(ve[s], k + 5)
                    nc.gpsimd.tensor_tensor(rrms[:, t], rtmp[:, 1, t], rstd[:, t], ALU.mult).then_inc(ve[s], 1)

        @block.scalar
        def _(act):
            for dst, src in loads:
                act.dma_start(dst, src).then_inc(ld_w, 16)
            act.wait_ge(ld_w, ALL_W)
            nc.scalar.copy(identb[:], ident[:]).then_inc(narrowed, 1)
            nc.scalar.copy(maskb[:], mask[:]).then_inc(narrowed, 1)
            nc.scalar.copy(masktb[:], maskt[:]).then_inc(narrowed, 1)

            def turn(s, g, scale=1.0):
                act.wait_ge(tr[s], g + 1)
                nc.scalar.activation(xT[:, G * g:G * (g + 1)], bank[g % 2][:], ACT.Copy, scale=scale).then_inc(xtr[s], 1)

            def recurrent_gates(g):
                act.wait_ge(proj0, g + 1)
                if g >= 2:
                    act.wait_ge(scanned, g - 1)
                for w, (dst, func) in enumerate(((sig, ACT.Sigmoid), (tnh, ACT.Tanh), (dec, ACT.Sigmoid))):
                    nc.scalar.activation(dst[:, g % 2, :], bank[2 + w][:], func,
                                         bias=rec_bias[:, w:w + 1]).then_inc(gates, 1)

            turn(0, 0)
            for g in range(NG):
                if g + 1 < NG:
                    turn(0, g + 1)
                recurrent_gates(g)
            for g in range(NG):
                turn(1, g, ns_sb[:, 0:1])
            act.wait_ge(gapr, 1)
            nc.scalar.activation(egap[:], gap[:], ACT.Exp).then_inc(egr, 1)
            for u in range(NE * NG * HC):
                act.wait_ge(up, u + 1)
                if u >= 2:
                    act.wait_ge(hd, u - 1)
                nc.scalar.activation(silu[:, u % 2, :], bank[2 + 2 * (u % 2)][:], ACT.Silu).then_inc(si, 1)
            for g in range(NG):
                turn(2, g)
            for t in range(NT):
                act.wait_ge(vp, t + 1)
                nc.scalar.copy(vals[:, t, :, 0:HD], bank[2 + t % 2][:].rearrange("p (h d) -> p h d", h=NH)).then_inc(vr, 1)
            for n in range(NHD):
                for k, (g, j, q0, w) in enumerate(STEPS):
                    u = NS * n + k
                    act.wait_ge(st, u + 1)
                    if u >= PT_RING:
                        act.wait_ge(pv, u - PT_RING + 1)
                    nc.scalar.activation(pt[:, u % PT_RING, 0:w], bank[2 + u % 2][:, 0:w], ACT.Exp,
                                         scale=HD ** -0.5).then_inc(ex, 1)
            for t in range(NT):
                act.wait_ge(ot, t + 1)
                if t >= 2:
                    act.wait_ge(yo, t - 1)
                nc.scalar.copy(attT[:, t % 2].rearrange("p c n -> p (c n)"), bank[t % 2][:]).then_inc(otr, 1)
            for g in range(NG):
                turn(3, g)
            for g in range(NG):
                b = g // GB
                act.wait_ge(ld_ffn[b], 32)
                for c in range(FC):
                    u = FC * g + c
                    act.wait_ge(h2, u + 1)
                    if g >= 2:
                        act.wait_ge(y2, g - 1)
                    nc.scalar.activation(hid2[:, g % 2, c, :], bank[2 + u % 2][:], ACT.Relu,
                                         bias=wffn_sb[:, b, FF + FC * D + c:FF + FC * D + c + 1]).then_inc(h2r, 1)

        @block.vector
        def _(dve):
            links = [0]

            def link(ins):
                links[0] += 1
                ins.then_inc(dvs, 1)
                dve.wait_ge(dvs, links[0])

            def norm_stats(s, b):
                for t in range(TB * b, TB * (b + 1)):
                    nc.vector.bn_stats(stats[:, t, :], xres[:, t, :]).then_inc(bn[s], 1)
                dve.wait_ge(bn[s], TB * (b + 1))
                for t in range(TB * b, TB * (b + 1)):
                    nc.vector.bn_aggr(mv[:, t, :], stats[:, t, :]).then_inc(mvr[s], 1)

            def norm_apply(s, b):
                dve.wait_ge(rs[s], b + 1)
                dve.wait_ge(mvr[s], TB * (b + 1))
                for t in range(TB * b, TB * (b + 1)):
                    nc.vector.tensor_scalar(xn[:, t, :], xres[:, t, :], mv[:, t, 0:1], rstd[:, t:t + 1],
                                            ALU.subtract, ALU.mult).then_inc(xnr[s], 1)

            for b in range(B):
                dve.wait_ge(ld_x[b], 16 * GB)
                norm_stats(0, b)
            for b in range(B):
                norm_apply(0, b)

            def residual1(g):
                dve.wait_ge(back, g + 1)
                tg = slice(TG * g, TG * (g + 1))
                nc.vector.tensor_tensor(xres[:, tg, :], xres[:, tg, :],
                                        bank[g % 2][:].rearrange("p (t d) -> p t d", t=TG), ALU.add).then_inc(res1, 1)

            for g in range(NG):
                dve.wait_ge(gates, 3 * (g + 1))
                nc.vector.tensor_tensor(scan_in[:, g % 2, :], sig[:, g % 2, :], tnh[:, g % 2, :], ALU.mult).then_inc(dvs, 1)
                nc.vector.tensor_scalar(dec[:, g % 2, :], dec[:, g % 2, :], 0.998, 0.001, ALU.mult, ALU.add).then_inc(dvs, 1)
                links[0] += 2
                dve.wait_ge(dvs, links[0])
                if g % GB:
                    dve.wait_ge(scanned, g)
                first = 0.0 if g % GB == 0 else hT[:, G * g - 1:G * g]
                nc.vector.tensor_tensor_scan(hT[:, G * g:G * (g + 1)], dec[:, g % 2, :], scan_in[:, g % 2, :], first,
                                             ALU.mult, ALU.add).then_inc(scanned, 1)
            for g in range(NG):
                residual1(g)

            for b in range(B):
                dve.wait_ge(res1, GB * (b + 1))
                norm_stats(1, b)
            for b in range(B):
                norm_apply(1, b)
                dve.wait_ge(ve[1], 6 * (b + 1))
                for t in range(TB * b, TB * (b + 1)):
                    nc.vector.tensor_scalar(xrms[:, t, :], xres[:, t, :], mv[:, t, 0:1], rrms[:, t:t + 1],
                                            ALU.subtract, ALU.mult).then_inc(rms, 1)

            dve.wait_ge(rout, 1)
            link(nc.vector.tensor_copy(scores[:], bank[6][:, 0:NT * NE].rearrange("p (t e) -> p t e", t=NT)))
            for t in range(NT):
                ins = nc.vector.max(top[:, t, :], scores[:, t, :])
            link(ins)
            for t in range(NT):
                ins = nc.vector.max_index(topi[:, t, :], top[:, t, :], scores[:, t, :])
            nc.vector.tensor_tensor(gap[:], top[:, :, 1], top[:, :, 0], ALU.subtract).then_inc(gapr, 1)
            link(ins)
            link(nc.vector.tensor_copy(topf[:], topi[:, :, 0:2]))
            for r in range(2):
                ins = nc.vector.tensor_tensor(chosen[:, r], iota[:].unsqueeze(1).to_broadcast([P, NT, NE]),
                                              topf[:, :, r:r + 1].to_broadcast([P, NT, NE]), ALU.is_equal)
            dve.wait_ge(egr, 1)
            link(nc.vector.tensor_scalar(prob[:, 1, :], egap[:], 1.0, None, ALU.add))
            link(nc.vector.reciprocal(prob[:, 0, :], prob[:, 1, :]))
            link(nc.vector.tensor_tensor(prob[:, 1, :], prob[:, 0, :], egap[:], ALU.mult))
            for r in range(2):
                ins = nc.vector.tensor_tensor(chosen[:, r], chosen[:, r],
                                              prob[:, r, :].unsqueeze(2).to_broadcast([P, NT, NE]), ALU.mult)
            link(ins)
            nc.vector.tensor_tensor(cw[:], chosen[:, 0], chosen[:, 1], ALU.add).then_inc(cwr, 1)
            dve.wait_ge(xnr[1], NT)
            link(nc.vector.tensor_tensor(xres[:], xres[:], xn[:], ALU.add))
            dve.wait_ge(cwr, 1)

            def combine(e, g):
                u = NG * e + g
                dve.wait_ge(dn, u + 1)
                if e:
                    dve.wait_ge(cmb, u - NG + 1)
                for i in range(TG):
                    t = TG * g + i
                    ins = nc.vector.scalar_tensor_tensor(xres[:, t, :], bank[6 + u % 2][:, D * i:D * (i + 1)],
                                                         cw[:, t, e:e + 1], xres[:, t, :], ALU.mult, ALU.add)
                ins.then_inc(cmb, 1)

            for e in range(NE):
                for g in range(NG):
                    for c in range(HC):
                        u = (e * NG + g) * HC + c
                        dve.wait_ge(si, u + 1)
                        if u >= 4:
                            dve.wait_ge(dn, u // HC - 1)
                        nc.vector.tensor_tensor(hid[:, u % 4, :], bank[3 + 2 * (u % 2)][:], silu[:, u % 2, :],
                                                ALU.mult).then_inc(hd, 1)
                    if e or g:
                        combine((e * NG + g - 1) // NG, (g - 1) % NG)
            combine(NE - 1, NG - 1)

            dve.wait_ge(cmb, NE * NG)
            for b in range(B):
                norm_stats(2, b)
            for b in range(B):
                norm_apply(2, b)

            def evacuate(pr, r):
                dve.wait_ge(pj, 4 * pr + r + 1)
                half = slice(G * (r % 2), G * (r % 2 + 1))
                for a in range(2):
                    rows = slice(HD * a, HD * (a + 1))
                    ins = nc.vector.tensor_tensor(qk[0:HD, pr % 2, a, r // 2, half], bank[6][rows, :], pe[rows, half], ALU.add)
                ins.then_inc(qkd, 1)

            def rounded(pr, a):
                dve.wait_ge(qkd, 4 * (pr + 1))
                if pr:
                    dve.wait_ge(mp, NC * (2 * (pr - 1) + a + 1))
                for r in range(2):
                    nc.vector.tensor_copy(qkr[0:HD, a, r, :], qk[0:HD, pr % 2, a, r, :]).then_inc(hi, 1)

            def max_chunk(n, m):
                i, c, w = CHUNKS[m]
                dve.wait_ge(mp, NC * n + m + 1)
                nc.vector.tensor_reduce(mx[:, n % 2, i, c:c + 1], bank[(NC * n + m) % 2][:, 0:w], AX_X,
                                        ALU.max).then_inc(mr, 1)

            def max_final(n):
                dve.wait_ge(mr, NC * (n + 1))
                nc.vector.tensor_reduce(mfin[:, n % 2, :], mx[:, n % 2], AX_X, ALU.max).then_inc(mf, 1)

            def max_row(n):
                dve.wait_ge(mt, n + 1)
                if n >= 2:
                    dve.wait_ge(mrow, 16 * (n - 1))
                nc.vector.tensor_scalar(nmt[:, n % 2, :], bank[7][0:TB, 0:P], -1.0, None, ALU.mult).then_inc(nm, 1)

            def normalise(n, g):
                b, h = n // NH, n % NH
                dve.wait_ge(pv, NS * n + (TG if g == 0 else NS))
                o = bank[4 + g][:, 0:TG * (HD + 1)].rearrange("p (t d) -> p t d", t=TG)
                nc.vector.reciprocal(rden[:, g, :], o[:, :, HD]).then_inc(den, 1)
                dve.wait_ge(den, 2 * n + g + 1)
                nc.vector.tensor_tensor(att[:, TB * b + TG * g:TB * b + TG * (g + 1), HD * h:HD * (h + 1)], o[:, :, 0:HD],
                                        rden[:, g, :].unsqueeze(2).to_broadcast([P, TG, HD]), ALU.mult).then_inc(on, 1)

            dve.wait_ge(consts, 4)
            dve.wait_ge(ld_w, ALL_W)
            for r in range(4):
                evacuate(0, r)
            rounded(0, 0)
            rounded(0, 1)
            for m in range(NC):
                max_chunk(0, m)
            max_final(0)
            max_row(0)
            for n in range(NHD):
                pr = n // 2 + 1
                nxt = n % 2 == 0 and pr < NP
                for k in range(NS):
                    if n + 1 < NHD:
                        for m in MAX_AT[k]:
                            max_chunk(n + 1, m)
                        if k == 8:
                            max_final(n + 1)
                        if k == 9:
                            max_row(n + 1)
                    if nxt and k in PROJ_AT:
                        evacuate(pr, PROJ_AT[k])
                    if nxt and k == 9:
                        rounded(pr, 0)
                    if nxt and k == 10:
                        rounded(pr, 1)
                    if k == 5:
                        normalise(n, 0)
                normalise(n, 1)

            for g in range(NG):
                dve.wait_ge(yo, TG * (g + 1))
                tg = slice(TG * g, TG * (g + 1))
                nc.vector.tensor_tensor(xres[:, tg, :], xres[:, tg, :],
                                        bank[4 + g % 2][:].rearrange("p (t d) -> p t d", t=TG), ALU.add).then_inc(res3, 1)
                if g % GB == GB - 1:
                    dve.wait_ge(res3, g + 1)
                    norm_stats(3, g // GB)
                    norm_apply(3, g // GB)
            for b in range(B):
                dve.wait_ge(mn, b + 1)
                nc.vector.tensor_scalar(mean_sb[:, b:b + 1], bank[6 + b][:, 0:1], 1.0 / T, None, ALU.mult).then_inc(mnr, 1)
                dve.wait_ge(sc, b + 1)
                link(nc.vector.tensor_tensor(sc1[:, b, :], bank[6 + b][0:1, 8:8 + NE], br1_sb[:], ALU.add))
                nc.vector.max(top1[:, b, :], sc1[:, b, :]).then_inc(idx, 1)
                dve.wait_ge(idx, 2 * b + 1)
                nc.vector.max_index(top1i[:, b, :], top1[:, b, :], sc1[:, b, :]).then_inc(idx, 1)
            for g in range(NG):
                dve.wait_ge(y2, g + 1)
                tg = slice(TG * g, TG * (g + 1))
                nc.vector.tensor_tensor(xres[:, tg, :], xres[:, tg, :],
                                        bank[4 + g % 2][:].rearrange("p (t d) -> p t d", t=TG), ALU.add).then_inc(res4, 1)

        @block.tensor
        def _(pe_):
            mm = nc.tensor.matmul

            def turn(s, g, src):
                for i in range(TG):
                    t = TG * g + i
                    ins = nc.tensor.transpose(bank[g % 2][:, P * i:P * (i + 1)], src[:, t, :], ident[:])
                ins.then_inc(tr[s], 1)

            pe_.wait_ge(ld_w, ALL_W)

            def turn0(g):
                pe_.wait_ge(xnr[0], TG * (g + 1))
                if g >= 2:
                    pe_.wait_ge(xtr[0], g - 1)
                turn(0, g, xn)

            turn0(0)
            for g in range(NG):
                if g + 1 < NG:
                    turn0(g + 1)
                pe_.wait_ge(xtr[0], g + 1)
                if g:
                    pe_.wait_ge(gates, 3 * g)
                for w in range(3):
                    ins = mm(bank[2 + w][:], w_rec[:, w, :], xT[:, G * g:G * (g + 1)], start=True, stop=True)
                ins.then_inc(proj0, 1)
            for g in range(NG):
                pe_.wait_ge(scanned, g + 1)
                if g >= 2:
                    pe_.wait_ge(res1, g - 1)
                for i in range(TG):
                    t = TG * g + i
                    ins = nc.tensor.transpose(bank[g % 2][:, P * i:P * (i + 1)], hT[:, P * t:P * (t + 1)], ident[:])
                ins.then_inc(back, 1)

            for g in range(NG):
                pe_.wait_ge(rms, TG * (g + 1))
                pe_.wait_ge(res1, min(g + 3, NG))
                if g >= 2:
                    pe_.wait_ge(xtr[1], g - 1)
                turn(1, g, xrms)
            for g in range(NG):
                pe_.wait_ge(xtr[1], g + 1)
                for t in range(TG * g, TG * (g + 1)):
                    ins = mm(bank[6][:, NE * t:NE * (t + 1)], xT[:, P * t:P * (t + 1)], wr0_sb[:], start=True, stop=True)
            ins.then_inc(rout, 1)

            def expert_down(v):
                e, g = v // NG, v % NG
                pe_.wait_ge(hd, HC * (v + 1))
                if v == 0:
                    pe_.wait_ge(cwr, 1)
                if v >= 2:
                    pe_.wait_ge(cmb, v - 1)
                for c in range(HC):
                    for i in range(TG):
                        ins = mm(bank[6 + v % 2][:, D * i:D * (i + 1)], hid[:, (HC * v + c) % 4, P * i:P * (i + 1)],
                                 wexp_sb[:, e % 2, 2 * HID + D * c:2 * HID + D * (c + 1)],
                                 start=(c == 0 and i == 0), stop=(c == HC - 1), skip_group_check=True)
                ins.then_inc(dn, 1)

            for e in range(NE):
                pe_.wait_ge(ld_exp[e % 2], 16 * (e // 2 + 1))
                for g in range(NG):
                    for c in range(HC):
                        u = (e * NG + g) * HC + c
                        if u >= 2:
                            pe_.wait_ge(hd, u - 1)
                        for w in range(2):
                            f = HID * (1 - w) + P * c
                            ins = mm(bank[2 + 2 * (u % 2) + w][:], wexp_sb[:, e % 2, f:f + P], xT[:, G * g:G * (g + 1)],
                                     start=True, stop=True)
                        ins.then_inc(up, 1)
                    if e or g:
                        expert_down(e * NG + g - 1)
            expert_down(NE * NG - 1)

            for g in range(NG):
                pe_.wait_ge(xnr[2], TG * (g + 1))
                if g >= 2:
                    pe_.wait_ge(xtr[2], g - 1)
                turn(2, g, xn)
            for t in range(NT):
                pe_.wait_ge(xtr[2], t // TG + 1)
                if t >= 2:
                    pe_.wait_ge(vr, t - 1)
                mm(bank[2 + t % 2][:], xT[:, P * t:P * (t + 1)], wv_sb[:], start=True, stop=True).then_inc(vp, 1)
            pe_.wait_ge(vr, NT)
            pe_.wait_ge(consts, 4)
            pe_.wait_ge(narrowed, 3)
            pe_.wait_ge(krow, 4)

            def project(pr, r):
                b, col = pr // (NH // 2), P * (r // 2)
                if pr or r:
                    pe_.wait_ge(qkd, 4 * pr + r)
                tok = T * b + G * (r % 2)
                mm(bank[6][:], wqk_sb[:, pr % (NH // 2), col:col + P], xT[:, tok:tok + G], start=True, stop=True).then_inc(pj, 1)

            def max_chunk(n, m):
                i, c, w = CHUNKS[m]
                u = NC * n + m
                last = c == i // TG
                if m == 0:
                    pe_.wait_ge(hi, 4 * (n // 2) + 2 * (n % 2) + 2)
                if u >= 2:
                    pe_.wait_ge(mr, u - 1)
                ins = mm(bank[u % 2][:, 0:w], qkr[0:HD, n % 2, 0, P * i:P * (i + 1)],
                         qkr[0:HD, n % 2, 1, G * c:G * c + w], start=True, stop=True)
                if last:
                    ins = mm(bank[u % 2][:, w - P:w], identb[:], maskb[:], start=False, stop=True, skip_group_check=True)
                ins.then_inc(mp, 1)

            def max_turn(n):
                pe_.wait_ge(mf, n + 1)
                if n:
                    pe_.wait_ge(nm, n)
                nc.tensor.transpose(bank[7][0:TB, 0:P], mfin[:, n % 2, :], ident[:]).then_inc(mt, 1)

            def score(n, k):
                g, j, q0, w = STEPS[k]
                u = NS * n + k
                pr, a = n // 2, n % 2
                if k == 0:
                    pe_.wait_ge(mrow, 16 * (n + 1))
                if u >= 2:
                    pe_.wait_ge(ex, u - 1)
                diag = q0 == P * j
                ins = mm(bank[2 + u % 2][:, 0:w], qk[0:HD + 1, pr % 2, a, 1, P * j:P * (j + 1)],
                         qk[0:HD + 1, pr % 2, a, 0, q0:q0 + w], start=True, stop=True)
                if diag:
                    ins = mm(bank[2 + u % 2][:, 0:P], identb[:], masktb[:], start=False, stop=True, skip_group_check=True)
                ins.then_inc(st, 1)

            def weigh(n, k):
                g, j, q0, w = STEPS[k]
                u = NS * n + k
                b, h = n // NH, n % NH
                pe_.wait_ge(ex, u + 1)
                if j == 0 and n:
                    pe_.wait_ge(on, 2 * (n - 1) + g + 1)
                for i in range(w // P):
                    at = (q0 - G * g) // P + i
                    ins = mm(bank[4 + g][:, (HD + 1) * at:(HD + 1) * (at + 1)], pt[:, u % PT_RING, P * i:P * (i + 1)],
                             vals[:, TB * b + j, h, :], start=(j == 0 and i == 0), stop=(j == TG * g + at),
                             skip_group_check=True)
                ins.then_inc(pv, 1)

            for r in range(4):
                project(0, r)
            for m in range(NC):
                max_chunk(0, m)
            max_turn(0)
            for n in range(NHD):
                pr = n // 2 + 1
                nxt = n % 2 == 0 and pr < NP
                for k in range(NS):
                    score(n, k)
                    if k:
                        weigh(n, k - 1)
                    elif n:
                        weigh(n - 1, NS - 1)
                    if n + 1 < NHD:
                        for m in MAX_AT[k]:
                            max_chunk(n + 1, m)
                        if k == 8:
                            max_turn(n + 1)
                    if nxt and k in PROJ_AT:
                        project(pr, PROJ_AT[k])
            weigh(NHD - 1, NS - 1)

            def turn_out(t):
                b = t // TB
                pe_.wait_ge(on, 2 * NH * (b + 1))
                if t >= 2:
                    pe_.wait_ge(otr, t - 1)
                for c in range(FC):
                    ins = nc.tensor.transpose(bank[t % 2][:, P * c:P * (c + 1)], att[:, t, P * c:P * (c + 1)], ident[:])
                ins.then_inc(ot, 1)

            turn_out(0)
            for t in range(NT):
                if t + 1 < NT:
                    turn_out(t + 1)
                g, i = t // TG, t % TG
                pe_.wait_ge(otr, t + 1)
                if t == 0:
                    pe_.wait_ge(on, 2 * NHD)
                if g >= 2 and i == 0:
                    pe_.wait_ge(res3, g - 1)
                for c in range(FC):
                    ins = mm(bank[4 + g % 2][:, D * i:D * (i + 1)], attT[:, t % 2, c, :], wo_sb[:, c, :],
                             start=(c == 0), stop=(c == FC - 1))
                ins.then_inc(yo, 1)

            for g in range(NG):
                pe_.wait_ge(xnr[3], TG * (g + 1))
                if g >= 2:
                    pe_.wait_ge(xtr[3], g - 1)
                turn(3, g, xn)
                if g % GB == GB - 1:
                    b = g // GB
                    for t in range(TB * b, TB * (b + 1)):
                        ins = mm(bank[6 + b][:, 0:1], xn[:, t, :], ones[:, 0:1], start=(t == TB * b), stop=(t == TB * (b + 1) - 1))
                    ins.then_inc(mn, 1)
                    pe_.wait_ge(mnr, b + 1)
                    mm(bank[6 + b][0:1, 8:8 + NE], mean_sb[:, b:b + 1], wr1_sb[:], start=True, stop=True).then_inc(sc, 1)
            for g in range(NG):
                b = g // GB
                pe_.wait_ge(xtr[3], g + 1)
                pe_.wait_ge(ld_ffn[b], 32)
                for c in range(FC):
                    u = FC * g + c
                    if u >= 2:
                        pe_.wait_ge(h2r, u - 1)
                    mm(bank[2 + u % 2][:], wffn_sb[:, b, P * c:P * (c + 1)], xT[:, G * g:G * (g + 1)],
                       start=True, stop=True).then_inc(h2, 1)
                if g >= 2:
                    pe_.wait_ge(res4, g - 1)
                pe_.wait_ge(h2r, FC * (g + 1))
                for i in range(TG):
                    dst = bank[4 + g % 2][:, D * i:D * (i + 1)]
                    for c in range(FC):
                        mm(dst, hid2[:, g % 2, c, P * i:P * (i + 1)], wffn_sb[:, b, FF + D * c:FF + D * (c + 1)],
                           start=(c == 0), stop=False)
                    ins = mm(dst, ones[0:1, :], b2_sb[:, b, :], start=False, stop=True)
                ins.then_inc(y2, 1)


def kernel(L0_attn_x, L0_attn_Wg, L0_attn_bg, L0_attn_Wv, L0_attn_bv, L0_attn_Wd, L0_attn_bd, L0_ffn_norm_scale,
           L0_ffn_w_router, L0_ffn_w_up, L0_ffn_w_down, L1_attn_Wqkv, L1_attn_Wo, L1_ffn_Wr, L1_ffn_br, L1_ffn_W1,
           L1_ffn_b1, L1_ffn_W2, L1_ffn_b2):
    import numpy as np
    import concourse.bacc as bacc
    from concourse.bass_utils import run_bass_kernel_spmd

    def arr(a):
        return np.ascontiguousarray(np.asarray(a))

    wqkv = arr(L1_attn_Wqkv).reshape(NH // 2, 2, 3, HD, D)
    wqk = wqkv[:, :, 0:2].transpose(4, 0, 2, 1, 3).reshape(D, NH // 2, 2 * P)
    wv = wqkv[:, :, 2].transpose(3, 0, 1, 2).reshape(D, NH * HD)
    w_up = arr(L0_ffn_w_up).transpose(0, 2, 1)
    w_down = arr(L0_ffn_w_down).reshape(NE, D, HC, P).transpose(0, 3, 2, 1).reshape(NE, P, HC * D)
    w2 = arr(L1_ffn_W2).reshape(NE, FC, P, D).transpose(0, 2, 1, 3).reshape(NE, P, FC * D)
    b1 = arr(L1_ffn_b1).reshape(NE, FC, P).transpose(0, 2, 1)

    pos = np.arange(T, dtype=np.float32)[:, None]
    div = np.exp(np.arange(0, HD, 2, dtype=np.float32) * np.float32(-np.log(10000.0) / HD)).astype(np.float32)
    ang = (pos * div).astype(np.float32)
    table = np.stack([np.sin(ang), np.cos(ang)], axis=-1).reshape(T, HD).astype(np.float32)
    late = np.triu(np.full((P, P), -3.0e38, np.float32), 1)

    arrays = {
        "x": arr(L0_attn_x).reshape(B * T, D), "wg": arr(L0_attn_Wg), "wv0": arr(L0_attn_Wv), "wd": arr(L0_attn_Wd),
        "gate_bias": np.stack([arr(L0_attn_bg), arr(L0_attn_bv), arr(L0_attn_bd)], axis=1),
        "ns": arr(L0_ffn_norm_scale).reshape(D, 1), "wr0": arr(L0_ffn_w_router).T,
        "wexp": np.concatenate([w_up, w_down], axis=2), "wqk": wqk, "wv": wv,
        "wo": arr(L1_attn_Wo).T.reshape(FC, P, D).transpose(1, 0, 2), "wr1": arr(L1_ffn_Wr),
        "br1": arr(L1_ffn_br).reshape(1, NE),
        "wffn": np.concatenate([arr(L1_ffn_W1), w2, b1], axis=2), "b2": arr(L1_ffn_b2),
        "ident_d": np.eye(P, dtype=np.float32), "mask_d": late, "maskt_d": late.T,
        "pe_d": np.concatenate([table.T, table.T], axis=0),
        "iota_d": np.tile(np.arange(NE, dtype=np.float32), (P, 1)),
    }
    arrays = {k: np.ascontiguousarray(v) for k, v in arrays.items()}
    nc = bacc.Bacc("TRN2", target_bir_lowering=False, num_devices=1)
    args = [nc.dram_tensor(k, v.shape, mybir.dt.from_np(v.dtype), kind="ExternalInput").ap() for k, v in arrays.items()]
    args.append(nc.dram_tensor("out", (B * T, D), F32, kind="ExternalOutput").ap())
    mixed_layers_kernel(nc, *args)
    r = run_bass_kernel_spmd(nc, [arrays], core_ids=[0])
    return r.results[0]["out"].reshape(B, T, D)
```

```python
import math
from contextlib import ExitStack

import concourse.bass as bass
from concourse import mybir

F32 = mybir.dt.float32
F32R = mybir.dt.float32r
BF16 = mybir.dt.bfloat16
F16 = mybir.dt.float16
U32 = mybir.dt.uint32
ALU = mybir.AluOpType
ACT = mybir.ActivationFunctionType
AX_X = mybir.AxisListType.X

P = 128
D = 128
B, T = 2, 1024
NT = B * T // P
TB = T // P
G = 512
NG = B * T // G
GB = T // G
TG = G // P
EPS_LN, EPS_RMS = 1e-5, 1e-6
NE, HID = 8, 256
HC = HID // P
NH, HD = 8, 64
NP = B * NH // 2
NHD = B * NH
FF = 512
FC = FF // P
PT_RING = 5
P32_RING = 3
VONE = HD
VREST = HD + 1
VCOLS = 2 * HD + 2
P_SCALE = 16.0
V_SCALE = 1024.0
SCORE_BANKS = (2, 3, 7)
LAG = 3

STEPS = [(g, j, max(G * g, P * j), G * (g + 1) - max(G * g, P * j)) for g in range(GB) for j in range(TG * (g + 1))]
NS = len(STEPS)
HALF = (slice(0, HD), slice(HD, 2 * HD))
SHIFT_ROW = (HD, 0)
WITH_SHIFT = (slice(0, HD + 1), slice(0, 2 * HD))
POOL_STEPS = (0, 4, 6, 8)
CHUNKS = [(i, c, min(G, P * (i + 1) - G * c)) for i in range(TB) for c in range(i // TG + 1)]
NC = len(CHUNKS)
MAX_AT = [[0], [1], [2], [3], [4, 5], [6, 7], [8, 9], [10, 11], [], [], [], []]
PROJ_AT = {0: 0, 1: 1, 3: 2, 4: 3}
ROUND_AT = {4: (0, 0), 5: (0, 1), 6: (1, 0), 7: (1, 1)}

BESIDE = {
    1: {0: ("turn", 2), 2: ("turn", 3), 4: ("values", 8), 6: ("values", 9)},
    3: {0: ("values", 10), 2: ("values", 11), 4: ("values", 12), 6: ("values", 13)},
    5: {0: ("values", 14), 2: ("values", 15)},
    8: {5: ("out_turn", 0), 6: ("out", 0)},
    9: {0: ("out_turn", 1), 1: ("out", 1), 2: ("out_turn", 2), 3: ("out", 2), 4: ("out_turn", 3), 5: ("out", 3),
        6: ("out_turn", 4), 7: ("out", 4)},
    10: {5: ("out_turn", 5), 6: ("out", 5)},
    11: {0: ("out_turn", 6), 1: ("out", 6), 2: ("out_turn", 7), 3: ("out", 7)},
    12: {5: ("ffn_turn", 0), 6: ("ffn_turn", 1), 7: ("ffn_scores", 0)},
    13: {4: ("ffn_up", 0), 5: ("ffn_up", 1), 6: ("ffn_up", 2), 7: ("ffn_up", 3)},
    14: {0: ("ffn_up", 4), 1: ("ffn_up", 5), 2: ("ffn_up", 6), 3: ("ffn_up", 7),
         4: ("ffn_down", 0), 5: ("ffn_down", 1), 6: ("ffn_down", 2), 7: ("ffn_down", 3)},
    15: {0: ("ffn_down", 4), 1: ("ffn_down", 5), 2: ("ffn_down", 6), 3: ("ffn_down", 7)},
}


def mixed_layers_kernel(nc, x, wg, wv0, wd, gate_bias, ns, wr0, wexp, wqk, wv, wo, wr1, br1, wffn, b2,
                        ident_d, mask_d, maskt_d, pe_d, iota_d, out):
    with ExitStack() as ctx:
        def sb(name, shape, dt=F32):
            return ctx.enter_context(nc.sbuf_tensor(name, shape, dt))

        def pb(name):
            return ctx.enter_context(nc.psum_tensor(name, [P, G], F32))

        def sem(name):
            return ctx.enter_context(nc.semaphore(name))

        xres = sb("xres", [P, NT, D])
        xn = sb("xn", [P, NT, D])
        xT = sb("xT", [P, B * T])
        stats = sb("stats", [P, NT, 6])
        mv = sb("mv", [P, NT, 2])
        rstd = sb("rstd", [P, NT])
        rtmp = sb("rtmp", [P, 4, NT])
        rrms = sb("rrms", [P, NT])
        euler = sb("euler", [P, NT])
        mhalf = sb("mhalf", [P, NT])
        ident = sb("ident", [P, P])
        identb = sb("identb", [P, P], BF16)
        maskb = sb("maskb", [P, P], BF16)
        masktb = sb("masktb", [P, P], BF16)
        pe = sb("pe", [P, T])
        iota = sb("iota", [P, NE])
        ones = sb("ones", [P, P])
        rec_bias = sb("rec_bias", [P, 3])
        ns_sb = sb("ns_sb", [P, 1])
        wr0_sb = sb("wr0_sb", [P, NE])
        wexp_sb = sb("wexp_sb", [P, 2, 2 * HID + HC * D])
        wqk_sb = sb("wqk_sb", [P, NH // 2, 2 * P])
        wv_sb = sb("wv_sb", [P, NH * HD])
        wo_sb = sb("wo_sb", [P, FC, D])
        wr1_sb = sb("wr1_sb", [P, NE])
        br1_sb = sb("br1_sb", [1, NE])
        wffn0 = sb("wffn0", [P, FF + FC * D + FC])
        b2_sb = sb("b2_sb", [1, B, D])
        scores = sb("scores", [P, NT, NE])
        top = sb("top", [P, NT, 8])
        topi = sb("topi", [P, NT, 8], U32)
        topf = sb("topf", [P, NT, 2])
        gap = sb("gap", [P, NT])
        egap = sb("egap", [P, NT])
        prob = sb("prob", [P, 2, NT])
        chosen = sb("chosen", [P, 2, NT, NE])
        cw = sb("cw", [P, NT, NE])
        vals = sb("vals", [P, NT, NH, VCOLS], F16)
        qk = sb("qk", [P, 2, T])
        qs = sb("qs", [P, 2, 2, T], F32R)
        kd = sb("kd", [P, 2, 2, T], F32R)
        qm = sb("qm", [P, 2, 2, T], F32R)
        kl = sb("kl", [P, 2, 2, T], F32R)
        p32 = sb("p32", [P, P32_RING, G])
        ph = sb("ph", [P, PT_RING, G], F16)
        pl = sb("pl", [P, PT_RING, G], F16)
        vnorm = sb("vnorm", [P, 3, FC])
        before = p32[:].rearrange("p a n -> p (a n)")
        w_rec = before[:, 0:3 * D].rearrange("p (w n) -> p w n", w=3)
        mask, maskt = before[:, 3 * D:3 * D + P], before[:, 3 * D + P:3 * D + 2 * P]
        wv2 = before[:, 2 * G:3 * G]
        att = sb("att", [P, NT, NH * HD])
        mx = sb("mx", [P, 2, TB, 2])
        mfin = sb("mfin", [P, 2, TB])
        nmt = sb("nmt", [TB, 2, P], F32R)
        rden = sb("rden", [P, 2, TG])
        attT = wexp_sb[:].rearrange("p a n -> p (a n)")[:, 0:2 * FC * P].rearrange("p (a c n) -> p a c n", a=2, c=FC)
        tok_sum = sb("tok_sum", [P, NG])
        mean_sb = sb("mean_sb", [P, B])
        sc1 = sb("sc1", [1, B, NE])
        top1 = sb("top1", [1, B, 8])
        top1i = sb("top1i", [1, B, 8], U32)

        wffn_sb = (wffn0[:], qk[:].rearrange("p a n -> p (a n)")[:, 0:FF + FC * D + FC])
        early = att[:].rearrange("p t f -> p (t f)")
        sig = early[:, 0:2 * G].rearrange("p (a n) -> p a n", a=2)
        tnh = early[:, 2 * G:4 * G].rearrange("p (a n) -> p a n", a=2)
        dec = early[:, 4 * G:6 * G].rearrange("p (a n) -> p a n", a=2)
        scan_in = early[:, 6 * G:8 * G].rearrange("p (a n) -> p a n", a=2)
        hT = early[:, 8 * G:12 * G]
        silu = early[:, 0:2 * G].rearrange("p (a n) -> p a n", a=2)
        hid = early[:, 2 * G:6 * G].rearrange("p (a n) -> p a n", a=4)
        xrms = early[:, 12 * G:16 * G].rearrange("p (t d) -> p t d", t=NT)
        hid2 = early[:, 0:8 * G].rearrange("p (a c n) -> p a c n", a=2, c=FC)

        bank = [pb(f"bank{i}") for i in range(8)]

        ld_x, ld_rec, ld_w = [sem("ld_x0"), sem("ld_x1")], sem("ld_rec"), sem("ld_w")
        ld_exp = [sem("ld_exp0"), sem("ld_exp1")]
        ld_ffn = [sem("ld_ffn0"), sem("ld_ffn1")]
        consts, narrowed = sem("consts"), sem("narrowed")
        bn = [sem(f"bn{s}") for s in range(4)]
        mvr = [sem(f"mv{s}") for s in range(4)]
        ve, rrmsr = sem("ve"), sem("rrmsr")
        rs = [sem(f"rstd{s}") for s in range(4)]
        xnr = [sem(f"xn{s}") for s in range(4)]
        tr = [sem(f"tr{s}") for s in range(4)]
        xtr = [sem(f"xt{s}") for s in range(4)]
        proj0, gates = sem("proj0"), sem("gates")
        dvs, krow = sem("dvs"), sem("krow")
        scanned, back, res1 = sem("scanned"), sem("back"), sem("res1")
        rms, routed, skipped = sem("rms"), sem("routed"), sem("skipped")
        rout, gapr, egr, cwr = sem("rout"), sem("gapr"), sem("egr"), sem("cwr")
        up, si, hd, dn, cmb = sem("up"), sem("si"), sem("hd"), sem("dn"), sem("cmb")
        vp, vr = sem("vp"), sem("vr")
        pj, qkd, hi, qlo, klo, dup = (sem(s) for s in ("pj", "qkd", "hi", "qlo", "klo", "dup"))
        mp, mr, mf, mt, nm, mrow = sem("mp"), sem("mr"), sem("mf"), sem("mt"), sem("nm"), sem("mrow")
        st, ex, pv, den, on = sem("st"), sem("ex"), sem("pv"), sem("den"), sem("on")
        pld, plp, vhr = sem("pld"), sem("plp"), sem("vhr")
        wsq, vn, vnp, vnr, vdg, vbc, wvr, wor = (sem(n) for n in ("wsq", "vn", "vnp", "vnr", "vdg", "vbc", "wvr", "wor"))
        ot, otr, yo, res3 = sem("ot"), sem("otr"), sem("yo"), sem("res3")
        mnr, sc, idx = sem("mnr"), sem("sc"), sem("idx")
        h2, h2r, y2, res4, stored = sem("h2"), sem("h2r"), sem("y2"), sem("res4"), sem("stored")

        x_v = x.rearrange("(t p) d -> p t d", p=P)
        out_v = out.rearrange("(t p) d -> p t d", p=P)
        loads_rec = [(ident[:], ident_d), (w_rec[:, 0, :], wg), (w_rec[:, 1, :], wv0), (w_rec[:, 2, :], wd),
                     (rec_bias[:], gate_bias)]
        loads = [(ns_sb[:], ns), (wr0_sb[:], wr0), (iota[:], iota_d), (mask[:], mask_d), (maskt[:], maskt_d),
                 (pe[:], pe_d), (wqk_sb[:], wqk), (wv_sb[:], wv), (wo_sb[:], wo), (wr1_sb[:], wr1), (br1_sb[:], br1)]
        ALL_REC, ALL_W = 16 * len(loads_rec), 16 * len(loads)

        block = ctx.enter_context(nc.Block())

        @block.sync
        def _(sp):
            for g in range(NG):
                sp.dma_start(xres[:, TG * g:TG * (g + 1), :], x_v[:, TG * g:TG * (g + 1), :]).then_inc(ld_x[g // GB], 16)
            for w in range(B * NE):
                if w >= 2:
                    sp.wait_ge(dn, (w - 1) * GB)
                sp.dma_start(wexp_sb[:, w % 2, :], wexp[w % NE]).then_inc(ld_exp[w % 2], 16)

            def copies(pr):
                for a in range(2):
                    sp.wait_ge(hi, 4 * pr + 2 * a + 2)
                    own, other = HALF[a], HALF[1 - a]
                    sp.dma_start(qm[own, pr % 2, a, :].bitcast(F32), qs[own, pr % 2, a, :].bitcast(F32)).then_inc(dup, 16)
                    sp.dma_start(kd[other, pr % 2, a, :].bitcast(F32), kd[own, pr % 2, a, :].bitcast(F32)).then_inc(dup, 16)

            def chosen_expert(b):
                sp.wait_ge(idx, 2 * (b + 1))
                e = sp.value_load(top1i[0:1, b, 0:1], min_val=0, max_val=NE - 1)
                sp.dma_start(wffn_sb[b], wffn[bass.ds(e, 1)].rearrange("a p n -> (a p) n")).then_inc(ld_ffn[b], 16)
                sp.dma_start(b2_sb[:, b, :], b2[bass.ds(e, 1), :]).then_inc(ld_ffn[b], 16)

            def store(g):
                sp.wait_ge(res4, g + 1)
                sp.dma_start(out_v[:, TG * g:TG * (g + 1), :], xres[:, TG * g:TG * (g + 1), :]).then_inc(stored, 16)

            copies(0)
            for n in range(NHD):
                sp.wait_ge(nm, n + 1)
                a, pr = n % 2, n // 2
                sp.dma_start(qm[SHIFT_ROW[a]:SHIFT_ROW[a] + 1, pr % 2, a, :].bitcast(F32), nmt[:, a, :].bitcast(F32)).then_inc(mrow, 16)
                if n % 2 and pr + 1 < NP:
                    copies(pr + 1)
                if n == 13:
                    chosen_expert(0)
            store(0)
            store(1)
            chosen_expert(1)
            store(2)
            store(3)
            sp.wait_ge(stored, 16 * NG)

        def probability_rest(engine, eng, n, k, done):
            u, w = NS * n + k, STEPS[k][3]
            eng.wait_ge(ex, u + 1)
            if u >= PT_RING:
                eng.wait_ge(pv, u - PT_RING + 1)
            engine.tensor_tensor(pl[:, u % PT_RING, 0:w], p32[:, u % P32_RING, 0:w], ph[:, u % PT_RING, 0:w],
                                 ALU.subtract).then_inc(done, 1)

        def rests(n, k):
            by_pool = n * len(POOL_STEPS) + sum(s <= k for s in POOL_STEPS)
            return by_pool, NS * n + k + 1 - by_pool

        @block.gpsimd
        def _(pool):
            nc.gpsimd.memset(mhalf[:], -0.5).then_inc(consts, 1)
            nc.gpsimd.memset(ones[:], 1.0).then_inc(consts, 1)
            nc.gpsimd.memset(vals[:, :, :, VONE:VONE + 1], 1.0).then_inc(consts, 1)
            nc.gpsimd.memset(mx[:], -3.0e38).then_inc(consts, 1)
            nc.gpsimd.memset(euler[:], math.e).then_inc(consts, 1)
            pool.wait_ge(consts, 5)
            for i, (dst, value) in enumerate(((qm[0:HD, :, 1, :], 0.0), (kl[0:HD, :, 1, :], 0.0), (kl[0:1, :, 1, :], 1.0),
                                              (kl[HD:HD + 1, :, 0, :], 1.0))):
                nc.gpsimd.memset(dst.bitcast(F32), value).then_inc(krow, 1)
                pool.wait_ge(krow, i + 1)

            def inverse_deviation(s, b):
                t = slice(TB * b, TB * (b + 1))
                pool.wait_ge(mvr[s], TB * (b + 1))
                nc.gpsimd.tensor_scalar_add(rtmp[:, 0, t], mv[:, t, 1], EPS_LN).then_inc(ve, 1)
                veq[0] += 1
                pool.wait_ge(ve, veq[0])
                nc.gpsimd.tensor_tensor(rstd[:, t], rtmp[:, 0, t], mhalf[:, t], ALU.pow).then_inc(rs[s], 1)
                pool.wait_ge(rs[s], b + 1)

            veq = [0]

            def linked(ins):
                veq[0] += 1
                ins.then_inc(ve, 1)
                pool.wait_ge(ve, veq[0])

            def inverse_rms(b):
                t = slice(TB * b, TB * (b + 1))
                linked(nc.gpsimd.tensor_tensor(rtmp[:, 1, t], rstd[:, t], rstd[:, t], ALU.mult))
                linked(nc.gpsimd.tensor_tensor(rtmp[:, 2, t], rtmp[:, 1, t], mv[:, t, 1], ALU.mult))
                linked(nc.gpsimd.tensor_scalar_add(rtmp[:, 3, t], rtmp[:, 2, t], EPS_RMS))
                linked(nc.gpsimd.tensor_tensor(rtmp[:, 1, t], rtmp[:, 3, t], mhalf[:, t], ALU.pow))
                nc.gpsimd.tensor_tensor(rrms[:, t], rtmp[:, 1, t], rstd[:, t], ALU.mult).then_inc(rrmsr, 1)
                pool.wait_ge(rrmsr, b + 1)

            def second_weight(b):
                t = slice(TB * b, TB * (b + 1))
                pool.wait_ge(gapr, b + 1)
                nc.gpsimd.tensor_tensor(egap[:, t], euler[:, t], gap[:, t], ALU.pow).then_inc(egr, 1)
                pool.wait_ge(egr, b + 1)

            def value_scales():
                pool.wait_ge(ld_w, ALL_W)
                nc.gpsimd.tensor_tensor(wv2[:], wv_sb[:], wv_sb[:], ALU.mult).then_inc(wsq, 1)
                pool.wait_ge(vnp, 1)
                nc.gpsimd.tensor_tensor(vnorm[:, 1, :], vnorm[:, 0, :], mhalf[:, 0:FC], ALU.pow).then_inc(vnr, 1)
                pool.wait_ge(vnr, 1)

            inverse_deviation(0, 0)
            inverse_deviation(0, 1)
            inverse_deviation(1, 0)
            inverse_rms(0)
            second_weight(0)
            inverse_deviation(1, 1)
            inverse_rms(1)
            second_weight(1)
            value_scales()
            inverse_deviation(2, 0)
            inverse_deviation(2, 1)

            def key_rest(pr, a):
                pool.wait_ge(hi, 4 * pr + 2 * a + 2)
                own = HALF[a]
                nc.gpsimd.tensor_tensor(kl[own, pr % 2, a, :], qk[own, 1, :], kd[own, pr % 2, a, :].bitcast(F32),
                                        ALU.subtract).then_inc(klo, 1)
                pool.wait_ge(klo, 2 * pr + a + 1)

            key_rest(0, 0)
            key_rest(0, 1)
            for n in range(NHD):
                for k in POOL_STEPS:
                    probability_rest(nc.gpsimd, pool, n, k, plp)
                    pool.wait_ge(plp, rests(n, k)[0])
                    if n % 2 and k == 4 and (n + 1) // 2 < NP:
                        key_rest((n + 1) // 2, 0)
                    if n % 2 and k == 6 and (n + 1) // 2 < NP:
                        key_rest((n + 1) // 2, 1)
                if n == 11:
                    inverse_deviation(3, 0)
            inverse_deviation(3, 1)

        @block.scalar
        def _(act):
            for dst, src in loads_rec:
                act.dma_start(dst, src).then_inc(ld_rec, 16)
            for dst, src in loads:
                act.dma_start(dst, src).then_inc(ld_w, 16)

            def turn(s, g, src, scale=1.0):
                act.wait_ge(tr[s], g + 1)
                nc.scalar.activation(xT[:, G * g:G * (g + 1)], src[:], ACT.Copy, scale=scale).then_inc(xtr[s], 1)

            def recurrent_gates(g):
                act.wait_ge(proj0, g + 1)
                if g >= 2:
                    act.wait_ge(scanned, g - 1)
                for w, (dst, func) in enumerate(((sig, ACT.Sigmoid), (tnh, ACT.Tanh), (dec, ACT.Sigmoid))):
                    nc.scalar.activation(dst[:, g % 2, :], bank[2 + w][:], func,
                                         bias=rec_bias[:, w:w + 1]).then_inc(gates, 1)

            def expert(w):
                for u in range(w * GB * HC, (w + 1) * GB * HC):
                    act.wait_ge(up, u + 1)
                    if u >= 2:
                        act.wait_ge(hd, u - 1)
                    nc.scalar.activation(silu[:, u % 2, :], bank[2 + 2 * (u % 2)][:], ACT.Silu).then_inc(si, 1)

            def values(t, src):
                act.wait_ge(vp, t + 1)
                nc.scalar.copy(vals[:, t, :, 0:HD], src[:].rearrange("p (h d) -> p h d", h=NH)).then_inc(vhr, 1)

            def out_turn(t, src):
                act.wait_ge(ot, t + 1)
                if t >= 2:
                    act.wait_ge(yo, t - 1)
                nc.scalar.copy(attT[:, t % 2].rearrange("p c n -> p (c n)"), src[:]).then_inc(otr, 1)

            def ffn_turn(g, src):
                act.wait_ge(tr[3], g + 1)
                nc.scalar.activation(xT[:, G * g:G * (g + 1)], src[:], ACT.Copy,
                                     accum_out=tok_sum[:, g:g + 1]).then_inc(xtr[3], 1)

            def ffn_up(u, src):
                g, c = u // FC, u % FC
                b = g // GB
                act.wait_ge(ld_ffn[b], 32)
                act.wait_ge(h2, u + 1)
                if g >= 2:
                    act.wait_ge(y2, g - 1)
                nc.scalar.activation(hid2[:, g % 2, c, :], src[:], ACT.Relu,
                                     bias=wffn_sb[b][:, FF + FC * D + c:FF + FC * D + c + 1]).then_inc(h2r, 1)

            act.wait_ge(ld_rec, ALL_REC)
            turn(0, 0, bank[0])
            turn(0, 1, bank[1])
            recurrent_gates(0)
            recurrent_gates(1)
            turn(0, 2, bank[0])
            turn(0, 3, bank[1])
            recurrent_gates(2)
            recurrent_gates(3)
            act.wait_ge(ld_w, ALL_W)
            turn(1, 0, bank[0], ns_sb[:, 0:1])
            turn(1, 1, bank[1], ns_sb[:, 0:1])
            expert(0)
            turn(1, 2, bank[0], ns_sb[:, 0:1])
            turn(1, 3, bank[1], ns_sb[:, 0:1])
            nc.scalar.copy(identb[:], ident[:]).then_inc(narrowed, 1)
            nc.scalar.copy(maskb[:], mask[:]).then_inc(narrowed, 1)
            nc.scalar.copy(masktb[:], maskt[:]).then_inc(narrowed, 1)
            for w in range(1, NE + 3):
                expert(w)
            turn(2, 0, bank[0])
            turn(2, 1, bank[1])
            for w in range(NE + 3, 2 * NE):
                expert(w)

            def round_half(pr, a, r):
                act.wait_ge(qkd, 4 * pr + 2 * r + 2)
                if pr:
                    act.wait_ge(st, NS * 2 * (pr - 1) + 1)
                dst = (qs, kd)[r]
                nc.scalar.copy(dst[HALF[a], pr % 2, a, :], qk[HALF[a], r, :]).then_inc(hi, 1)

            for a in range(2):
                for r in range(2):
                    round_half(0, a, r)
            for t in range(TB):
                values(t, bank[2 + t % 2])
            for n in range(NHD):
                for k, (g, j, q0, w) in enumerate(STEPS):
                    u = NS * n + k
                    act.wait_ge(st, u + 1)
                    if u >= PT_RING:
                        act.wait_ge(pv, u - PT_RING + 1)
                    if u >= P32_RING:
                        by_pool, by_vector = rests(*divmod(u - P32_RING, NS))
                        if (u - P32_RING) % NS in POOL_STEPS:
                            act.wait_ge(plp, by_pool)
                        else:
                            act.wait_ge(pld, by_vector)
                    nc.scalar.activation(ph[:, u % PT_RING, 0:w], bank[SCORE_BANKS[u % 3]][:, 0:w], ACT.Exp,
                                         scale=HD ** -0.5)
                    nc.scalar.activation(p32[:, u % P32_RING, 0:w], bank[SCORE_BANKS[u % 3]][:, 0:w], ACT.Exp,
                                         scale=HD ** -0.5).then_inc(ex, 1)
                    if n % 2 == 0 and n // 2 + 1 < NP and k in ROUND_AT:
                        round_half(n // 2 + 1, *ROUND_AT[k])
                    work, i = BESIDE.get(n, {}).get(k, ("", 0))
                    if work == "turn":
                        turn(2, i, bank[6])
                    elif work == "values":
                        values(i, bank[6])
                    elif work == "out_turn":
                        out_turn(i, bank[6])
                    elif work == "ffn_turn":
                        ffn_turn(i, bank[6])
                    elif work == "ffn_up":
                        ffn_up(i, bank[6])
            for t in range(TB, NT):
                out_turn(t, bank[t % 2])
            for g in range(GB, NG):
                ffn_turn(g, bank[g % 2])
            for u in range(FC * GB, FC * NG):
                ffn_up(u, bank[4 + u % 2])

        @block.vector
        def _(dve):
            links = [0]

            def link(ins):
                links[0] += 1
                ins.then_inc(dvs, 1)
                dve.wait_ge(dvs, links[0])

            def norm_stats(s, b):
                for t in range(TB * b, TB * (b + 1)):
                    nc.vector.bn_stats(stats[:, t, :], xres[:, t, :]).then_inc(bn[s], 1)
                dve.wait_ge(bn[s], TB * (b + 1))
                for t in range(TB * b, TB * (b + 1)):
                    nc.vector.bn_aggr(mv[:, t, :], stats[:, t, :]).then_inc(mvr[s], 1)

            def norm_apply(s, b):
                dve.wait_ge(rs[s], b + 1)
                dve.wait_ge(mvr[s], TB * (b + 1))
                for t in range(TB * b, TB * (b + 1)):
                    nc.vector.tensor_scalar(xn[:, t, :], xres[:, t, :], mv[:, t, 0:1], rstd[:, t:t + 1],
                                            ALU.subtract, ALU.mult).then_inc(xnr[s], 1)

            def residual(g, src, ready, value, done):
                dve.wait_ge(ready, value)
                tg = slice(TG * g, TG * (g + 1))
                nc.vector.tensor_tensor(xres[:, tg, :], xres[:, tg, :], src[:].rearrange("p (t d) -> p t d", t=TG),
                                        ALU.add).then_inc(done, 1)

            def scan(g):
                dve.wait_ge(gates, 3 * (g + 1))
                if g >= 2:
                    dve.wait_ge(scanned, g - 1)
                nc.vector.tensor_tensor(scan_in[:, g % 2, :], sig[:, g % 2, :], tnh[:, g % 2, :], ALU.mult).then_inc(dvs, 1)
                nc.vector.tensor_scalar(dec[:, g % 2, :], dec[:, g % 2, :], 0.998, 0.001, ALU.mult, ALU.add).then_inc(dvs, 1)
                links[0] += 2
                dve.wait_ge(dvs, links[0])
                if g % GB:
                    dve.wait_ge(scanned, g)
                first = 0.0 if g % GB == 0 else hT[:, G * g - 1:G * g]
                nc.vector.tensor_tensor_scan(hT[:, G * g:G * (g + 1)], dec[:, g % 2, :], scan_in[:, g % 2, :], first,
                                             ALU.mult, ALU.add).then_inc(scanned, 1)

            def rms_apply(b):
                dve.wait_ge(rrmsr, b + 1)
                for t in range(TB * b, TB * (b + 1)):
                    nc.vector.tensor_scalar(xrms[:, t, :], xres[:, t, :], mv[:, t, 0:1], rrms[:, t:t + 1],
                                            ALU.subtract, ALU.mult).then_inc(rms, 1)
                dve.wait_ge(xnr[1], TB * (b + 1))
                dve.wait_ge(rms, TB * (b + 1))
                tb = slice(TB * b, TB * (b + 1))
                nc.vector.tensor_tensor(xres[:, tb, :], xres[:, tb, :], xn[:, tb, :], ALU.add).then_inc(skipped, 1)

            def route(b):
                tb = slice(TB * b, TB * (b + 1))
                dve.wait_ge(rout, b + 1)
                nc.vector.tensor_copy(scores[:, tb, :], bank[0][:, 0:TB * NE].rearrange("p (t e) -> p t e", t=TB)).then_inc(routed, 1)
                dve.wait_ge(routed, b + 1)
                for t in range(TB * b, TB * (b + 1)):
                    ins = nc.vector.max(top[:, t, :], scores[:, t, :])
                link(ins)
                nc.vector.tensor_tensor(gap[:, tb], top[:, tb, 1], top[:, tb, 0], ALU.subtract).then_inc(gapr, 1)
                for t in range(TB * b, TB * (b + 1)):
                    ins = nc.vector.max_index(topi[:, t, :], top[:, t, :], scores[:, t, :])
                link(ins)
                link(nc.vector.tensor_copy(topf[:, tb, :], topi[:, tb, 0:2]))
                for r in range(2):
                    ins = nc.vector.tensor_tensor(chosen[:, r, tb], iota[:].unsqueeze(1).to_broadcast([P, TB, NE]),
                                                  topf[:, tb, r:r + 1].to_broadcast([P, TB, NE]), ALU.is_equal)
                dve.wait_ge(egr, b + 1)
                link(nc.vector.tensor_scalar(prob[:, 1, tb], egap[:, tb], 1.0, None, ALU.add))
                link(nc.vector.reciprocal(prob[:, 0, tb], prob[:, 1, tb]))
                link(nc.vector.tensor_tensor(prob[:, 1, tb], prob[:, 0, tb], egap[:, tb], ALU.mult))
                for r in range(2):
                    ins = nc.vector.tensor_tensor(chosen[:, r, tb], chosen[:, r, tb],
                                                  prob[:, r, tb].unsqueeze(2).to_broadcast([P, TB, NE]), ALU.mult)
                link(ins)
                nc.vector.tensor_tensor(cw[:, tb], chosen[:, 0, tb], chosen[:, 1, tb], ALU.add).then_inc(cwr, 1)

            def combine(v):
                w, g = v // GB, v // (NE * GB) * GB + v % GB
                dve.wait_ge(dn, v + 1)
                if w % NE == 0:
                    dve.wait_ge(cwr, w // NE + 1)
                    dve.wait_ge(skipped, w // NE + 1)
                else:
                    dve.wait_ge(cmb, v - GB + 1)
                for i in range(TG):
                    t = TG * g + i
                    ins = nc.vector.scalar_tensor_tensor(xres[:, t, :], bank[6 + v % 2][:, D * i:D * (i + 1)],
                                                         cw[:, t, w % NE:w % NE + 1], xres[:, t, :], ALU.mult, ALU.add)
                ins.then_inc(cmb, 1)

            def expert(w):
                for v in range(w * GB, (w + 1) * GB):
                    for u in range(v * HC, (v + 1) * HC):
                        dve.wait_ge(si, u + 1)
                        if u >= 4:
                            dve.wait_ge(dn, u // HC - 1)
                        nc.vector.tensor_tensor(hid[:, u % 4, :], bank[3 + 2 * (u % 2)][:], silu[:, u % 2, :],
                                                ALU.mult).then_inc(hd, 1)
                    if v:
                        combine(v - 1)

            for b in range(B):
                dve.wait_ge(ld_x[b], 16 * GB)
                norm_stats(0, b)
                if b:
                    norm_apply(0, b - 1)
            norm_apply(0, B - 1)
            scan(0)
            scan(1)
            for g in range(GB):
                residual(g, bank[g % 2], back, g + 1, res1)
            dve.wait_ge(res1, GB)
            norm_stats(1, 0)
            scan(2)
            scan(3)

            norm_apply(1, 0)
            rms_apply(0)
            route(0)
            for g in range(GB, NG):
                residual(g, bank[g % 2], back, g + 1, res1)
            dve.wait_ge(res1, NG)
            norm_stats(1, 1)
            expert(0)
            norm_apply(1, 1)
            rms_apply(1)
            expert(1)
            route(1)
            for w in range(2, NE + 1):
                expert(w)
                if w == 2:
                    dve.wait_ge(consts, 5)
                    dve.wait_ge(ld_w, ALL_W)
                    dve.wait_ge(vn, 1)
                    nc.vector.tensor_scalar(vnorm[:, 0, :], bank[1][:, 0:FC], D / V_SCALE ** 2, 1e-30, ALU.mult,
                                            ALU.add).then_inc(vnp, 1)
                elif w == 4:
                    dve.wait_ge(vnr, 1)
                    for c in range(FC):
                        ins = nc.vector.tensor_scalar(wv2[:, P * c:P * (c + 1)], ident[:], vnorm[:, 1, c:c + 1], None, ALU.mult)
                    ins.then_inc(vdg, 1)
                    link(nc.vector.reciprocal(vnorm[:, 2, :], vnorm[:, 1, :]))
                    for c in range(FC):
                        ins = nc.vector.tensor_scalar(wo_sb[:, c, :], wo_sb[:, c, :], vnorm[:, 2, c:c + 1], None, ALU.mult)
                    ins.then_inc(wor, 1)
                elif w == 5:
                    dve.wait_ge(vbc, 1)
                    nc.vector.tensor_tensor(wv_sb[:], wv_sb[:], bank[1][:], ALU.mult).then_inc(wvr, 1)
            dve.wait_ge(cmb, NE * GB)
            norm_stats(2, 0)
            expert(NE + 1)
            norm_apply(2, 0)
            for w in range(NE + 2, 2 * NE):
                expert(w)
            combine(2 * NE * GB - 1)
            dve.wait_ge(cmb, 2 * NE * GB)
            norm_stats(2, 1)

            def evacuate(pr, r):
                dve.wait_ge(pj, 4 * pr + r + 1)
                if pr:
                    dve.wait_ge(hi, 4 * pr)
                    dve.wait_ge(qlo, 2 * pr)
                    dve.wait_ge(klo, 2 * pr)
                half = slice(G * (r % 2), G * (r % 2 + 1))
                nc.vector.tensor_tensor(qk[:, r // 2, half], bank[6][:], pe[:, half], ALU.add).then_inc(qkd, 1)

            def query_rest(pr, a):
                dve.wait_ge(hi, 4 * pr + 2 * a + 1)
                own, other = HALF[a], HALF[1 - a]
                nc.vector.tensor_tensor(qs[other, pr % 2, a, :], qk[own, 0, :], qs[own, pr % 2, a, :].bitcast(F32),
                                        ALU.subtract).then_inc(qlo, 1)

            def max_chunk(n, m):
                i, c, w = CHUNKS[m]
                dve.wait_ge(mp, NC * n + m + 1)
                nc.vector.tensor_reduce(mx[:, n % 2, i, c:c + 1], bank[(NC * n + m) % 2][:, 0:w], AX_X,
                                        ALU.max).then_inc(mr, 1)

            def max_final(n):
                dve.wait_ge(mr, NC * (n + 1))
                nc.vector.tensor_reduce(mfin[:, n % 2, :], mx[:, n % 2], AX_X, ALU.max).then_inc(mf, 1)

            def max_row(n):
                dve.wait_ge(mt, n + 1)
                if n >= 2:
                    dve.wait_ge(mrow, 16 * (n - 1))
                nc.vector.tensor_scalar(nmt[:, n % 2, :], bank[6][0:TB, 0:P], -1.0,
                                        HD ** 0.5 * math.log(P_SCALE), ALU.mult, ALU.add).then_inc(nm, 1)

            def normalise(n, g):
                b, h = n // NH, n % NH
                dve.wait_ge(pv, NS * n + (TG if g == 0 else NS))
                o = bank[4 + g][:, 0:TG * (HD + 1)].rearrange("p (t d) -> p t d", t=TG)
                nc.vector.reciprocal(rden[:, g, :], o[:, :, HD]).then_inc(den, 1)
                dve.wait_ge(den, 2 * n + g + 1)
                nc.vector.tensor_tensor(att[:, TB * b + TG * g:TB * b + TG * (g + 1), HD * h:HD * (h + 1)], o[:, :, 0:HD],
                                        rden[:, g, :].unsqueeze(2).to_broadcast([P, TG, HD]), ALU.mult).then_inc(on, 1)

            def out_add(t, src):
                dve.wait_ge(yo, t + 1)
                nc.vector.tensor_tensor(xres[:, t, :], xres[:, t, :], src, ALU.add).then_inc(res3, 1)

            def best_expert(b):
                dve.wait_ge(xtr[3], GB * (b + 1))
                link(nc.vector.tensor_tensor(mean_sb[:, b:b + 1], tok_sum[:, GB * b:GB * b + 1],
                                             tok_sum[:, GB * b + 1:GB * b + 2], ALU.add))
                nc.vector.tensor_scalar(mean_sb[:, b:b + 1], mean_sb[:, b:b + 1], 1.0 / T, None, ALU.mult).then_inc(mnr, 1)
                dve.wait_ge(sc, b + 1)
                link(nc.vector.tensor_tensor(sc1[:, b, :], bank[6][0:1, 0:NE], br1_sb[:], ALU.add))
                nc.vector.max(top1[:, b, :], sc1[:, b, :]).then_inc(idx, 1)
                dve.wait_ge(idx, 2 * b + 1)
                nc.vector.max_index(top1i[:, b, :], top1[:, b, :], sc1[:, b, :]).then_inc(idx, 1)

            def value_rest(t, src):
                dve.wait_ge(vhr, t + 1)
                nc.vector.tensor_tensor(vals[:, t, :, VREST:VREST + HD], src[:].rearrange("p (h d) -> p h d", h=NH),
                                        vals[:, t, :, 0:HD], ALU.subtract).then_inc(vr, 1)

            for r in range(4):
                evacuate(0, r)
            query_rest(0, 0)
            query_rest(0, 1)
            for t in range(TB):
                value_rest(t, bank[2 + t % 2])
            for m in range(NC):
                max_chunk(0, m)
            max_final(0)
            max_row(0)
            for n in range(NHD):
                pr = n // 2 + 1
                nxt = n % 2 == 0 and pr < NP
                for k in range(NS):
                    if n + 1 < NHD:
                        for m in MAX_AT[k]:
                            max_chunk(n + 1, m)
                        if k == 8:
                            max_final(n + 1)
                        if k == 9:
                            max_row(n + 1)
                    if nxt and k in PROJ_AT:
                        evacuate(pr, PROJ_AT[k])
                    if k not in POOL_STEPS:
                        probability_rest(nc.vector, dve, n, k, pld)
                    if nxt and k in (9, 11):
                        query_rest(pr, (k - 9) // 2)
                    if k == TG - 1 + LAG:
                        normalise(n, 0)
                    if k == LAG - 1 and n:
                        normalise(n - 1, 1)
                    work, i = BESIDE.get(n, {}).get(k, ("", 0))
                    if work == "values":
                        value_rest(i, bank[6])
                    elif work == "out":
                        out_add(i, bank[6][:, 0:D])
                    elif work == "ffn_scores":
                        best_expert(i)
                    elif work == "ffn_down" and i % TG == TG - 1:
                        residual(i // TG, bank[6], y2, i // TG + 1, res4)
                    if (n, k) == (0, 10):
                        norm_apply(2, 1)
                    if (n, k) == (11, 8):
                        dve.wait_ge(res3, TB)
                        norm_stats(3, 0)
                    if (n, k) == (12, 3):
                        norm_apply(3, 0)
            normalise(NHD - 1, 1)

            for g in range(GB, NG):
                residual(g, bank[2 + g % 2], yo, TG * (g + 1), res3)
            dve.wait_ge(res3, TB + NG - GB)
            norm_stats(3, 1)
            norm_apply(3, 1)
            best_expert(1)
            for g in range(GB, NG):
                residual(g, bank[2 + g % 2], y2, g + 1, res4)

        @block.tensor
        def _(pe_):
            mm = nc.tensor.matmul

            def turn(s, g, src, dst):
                for i in range(TG):
                    t = TG * g + i
                    ins = nc.tensor.transpose(dst[:, P * i:P * (i + 1)], src[:, t, :], ident[:])
                ins.then_inc(tr[s], 1)

            def project0(g):
                pe_.wait_ge(xtr[0], g + 1)
                if g:
                    pe_.wait_ge(gates, 3 * g)
                for w in range(3):
                    ins = mm(bank[2 + w][:], w_rec[:, w, :], xT[:, G * g:G * (g + 1)], start=True, stop=True)
                ins.then_inc(proj0, 1)

            def turn_back(g):
                pe_.wait_ge(scanned, g + 1)
                for i in range(TG):
                    t = TG * g + i
                    ins = nc.tensor.transpose(bank[g % 2][:, P * i:P * (i + 1)], hT[:, P * t:P * (t + 1)], ident[:])
                ins.then_inc(back, 1)

            def turn1(g):
                pe_.wait_ge(rms, TG * (g + 1))
                pe_.wait_ge(res1, g + 1)
                turn(1, g, xrms, bank[g % 2])

            def route(b):
                pe_.wait_ge(xtr[1], GB * (b + 1))
                for t in range(TB):
                    tok = T * b + P * t
                    ins = mm(bank[0][:, NE * t:NE * (t + 1)], xT[:, tok:tok + P], wr0_sb[:], start=True, stop=True)
                ins.then_inc(rout, 1)

            pe_.wait_ge(ld_rec, ALL_REC)
            for b in range(B):
                for g in range(GB * b, GB * (b + 1)):
                    pe_.wait_ge(xnr[0], TG * (g + 1))
                    if b:
                        pe_.wait_ge(xtr[0], g - 1)
                    turn(0, g, xn, bank[g % 2])
                for g in range(GB * b, GB * (b + 1)):
                    project0(g)
            pe_.wait_ge(xtr[0], NG)
            turn_back(0)
            turn_back(1)
            turn1(0)
            turn1(1)
            pe_.wait_ge(ld_w, ALL_W)
            route(0)
            pe_.wait_ge(routed, 1)
            turn_back(2)
            turn_back(3)

            def expert_down(v):
                w = v // GB
                pe_.wait_ge(hd, HC * (v + 1))
                if v >= 2:
                    pe_.wait_ge(cmb, v - 1)
                for c in range(HC):
                    for i in range(TG):
                        ins = mm(bank[6 + v % 2][:, D * i:D * (i + 1)], hid[:, (HC * v + c) % 4, P * i:P * (i + 1)],
                                 wexp_sb[:, w % 2, 2 * HID + D * c:2 * HID + D * (c + 1)],
                                 start=(c == 0 and i == 0), stop=(c == HC - 1), skip_group_check=True)
                ins.then_inc(dn, 1)

            def expert(w):
                pe_.wait_ge(ld_exp[w % 2], 16 * (w // 2 + 1))
                for v in range(w * GB, (w + 1) * GB):
                    g = w // NE * GB + v % GB
                    for c in range(HC):
                        u = v * HC + c
                        if u >= 2:
                            pe_.wait_ge(hd, u - 1)
                        for r in range(2):
                            f = HID * (1 - r) + P * c
                            ins = mm(bank[2 + 2 * (u % 2) + r][:], wexp_sb[:, w % 2, f:f + P], xT[:, G * g:G * (g + 1)],
                                     start=True, stop=True)
                        ins.then_inc(up, 1)
                    if v:
                        expert_down(v - 1)

            pe_.wait_ge(gates, 3 * NG)
            expert(0)
            turn1(2)
            turn1(3)
            route(1)
            for w in range(1, NE + 3):
                expert(w)
                if w == 1:
                    pe_.wait_ge(wsq, 1)
                    pe_.wait_ge(consts, 5)
                    pe_.wait_ge(xtr[1], NG)
                    for c in range(FC):
                        ins = mm(bank[1][:, c:c + 1], wv2[:, P * c:P * (c + 1)], ones[:, 0:1], start=True, stop=True)
                    ins.then_inc(vn, 1)
                elif w == 4:
                    pe_.wait_ge(vdg, 1)
                    for c in range(FC):
                        ins = mm(bank[1][:, P * c:P * (c + 1)], ones[:], wv2[:, P * c:P * (c + 1)], start=True, stop=True)
                    ins.then_inc(vbc, 1)
            pe_.wait_ge(routed, 2)
            pe_.wait_ge(wvr, 1)
            for g in range(GB):
                pe_.wait_ge(xnr[2], TG * (g + 1))
                turn(2, g, xn, bank[g % 2])
            for w in range(NE + 3, 2 * NE):
                expert(w)
            expert_down(2 * NE * GB - 1)

            def values(t, dst):
                mm(dst[:], xT[:, P * t:P * (t + 1)], wv_sb[:], start=True, stop=True).then_inc(vp, 1)

            last = []

            def shared_bank(work, i):
                if last:
                    before, n = last.pop()
                    if before == "project":
                        pe_.wait_ge(qkd, n + 1)
                    elif before == "max_turn":
                        pe_.wait_ge(nm, n + 1)
                    elif before == "turn":
                        pe_.wait_ge(xtr[2], n + 1)
                    elif before == "values":
                        pe_.wait_ge(vr, n + 1)
                    elif before == "out_turn":
                        pe_.wait_ge(otr, n + 1)
                    elif before == "out":
                        pe_.wait_ge(res3, n + 1)
                    elif before == "ffn_turn":
                        pe_.wait_ge(xtr[3], n + 1)
                    elif before == "ffn_scores":
                        pe_.wait_ge(idx, 2 * n + 1)
                    elif before == "ffn_up":
                        pe_.wait_ge(h2r, n + 1)
                    elif before == "ffn_down" and n % TG == TG - 1:
                        pe_.wait_ge(res4, n // TG + 1)
                last.append((work, i))

            def project(pr, r):
                b, col = pr // (NH // 2), P * (r // 2)
                shared_bank("project", 4 * pr + r)
                tok = T * b + G * (r % 2)
                mm(bank[6][:], wqk_sb[:, pr % (NH // 2), col:col + P], xT[:, tok:tok + G], start=True, stop=True).then_inc(pj, 1)

            def max_chunk(n, m):
                i, c, w = CHUNKS[m]
                u = NC * n + m
                last = c == i // TG
                pr, a = n // 2, n % 2
                own = HALF[a]
                if m == 0:
                    pe_.wait_ge(hi, 4 * (n // 2) + 2 * (n % 2) + 2)
                if u >= 2:
                    pe_.wait_ge(mr, u - 1)
                ins = mm(bank[u % 2][:, 0:w], qs[own, pr % 2, a, P * i:P * (i + 1)],
                         kd[own, pr % 2, a, G * c:G * c + w], start=True, stop=True)
                if last:
                    ins = mm(bank[u % 2][:, w - P:w], identb[:], maskb[:], start=False, stop=True, skip_group_check=True)
                ins.then_inc(mp, 1)

            def max_turn(n):
                pe_.wait_ge(mf, n + 1)
                shared_bank("max_turn", n)
                nc.tensor.transpose(bank[6][0:TB, 0:P], mfin[:, n % 2, :], ident[:]).then_inc(mt, 1)

            def score(n, k):
                g, j, q0, w = STEPS[k]
                u = NS * n + k
                pr, a = n // 2, n % 2
                if k == 0:
                    pe_.wait_ge(mrow, 16 * (n + 1))
                if k == 0 and a == 0:
                    pe_.wait_ge(dup, 64 * (pr + 1))
                    pe_.wait_ge(qlo, 2 * (pr + 1))
                    pe_.wait_ge(klo, 2 * (pr + 1))
                if u >= 3:
                    pe_.wait_ge(ex, u - 2)
                diag = q0 == P * j
                dst = bank[SCORE_BANKS[u % 3]]
                keys, queries, rows = slice(P * j, P * (j + 1)), slice(q0, q0 + w), WITH_SHIFT[a]
                mm(dst[:, 0:w], kd[:, pr % 2, a, keys], qs[:, pr % 2, a, queries], start=True, stop=False)
                ins = mm(dst[:, 0:w], kl[rows, pr % 2, a, keys], qm[rows, pr % 2, a, queries], start=False, stop=True)
                if diag:
                    ins = mm(dst[:, 0:P], identb[:], masktb[:], start=False, stop=True, skip_group_check=True)
                ins.then_inc(st, 1)

            def weigh(n, k):
                g, j, q0, w = STEPS[k]
                u = NS * n + k
                b, h = n // NH, n % NH
                pe_.wait_ge(ex, u + 1)
                by_pool, by_vector = rests(n, k)
                if k in POOL_STEPS:
                    pe_.wait_ge(plp, by_pool)
                else:
                    pe_.wait_ge(pld, by_vector)
                if j == 0 and n:
                    pe_.wait_ge(on, 2 * (n - 1) + g + 1)
                for i in range(w // P):
                    at = (q0 - G * g) // P + i
                    dst = bank[4 + g][:, (HD + 1) * at:(HD + 1) * (at + 1)]
                    rounded, rest = ph[:, u % PT_RING, P * i:P * (i + 1)], pl[:, u % PT_RING, P * i:P * (i + 1)]
                    v = vals[:, TB * b + j, h, :]
                    mm(dst, rounded, v[:, 0:HD + 1], start=(j == 0 and i == 0), stop=False, skip_group_check=True)
                    mm(dst[:, 0:HD], rounded, v[:, VREST:VREST + HD], start=False, stop=False, skip_group_check=True)
                    ins = mm(dst, rest, v[:, 0:HD + 1], start=False, stop=(j == TG * g + at), skip_group_check=True)
                ins.then_inc(pv, 1)

            def out_turn(t, dst):
                for c in range(FC):
                    ins = nc.tensor.transpose(dst[:, P * c:P * (c + 1)], att[:, t, P * c:P * (c + 1)], ident[:])
                ins.then_inc(ot, 1)

            def out_project(t, dst):
                pe_.wait_ge(otr, t + 1)
                pe_.wait_ge(wor, 1)
                for c in range(FC):
                    ins = mm(dst, attT[:, t % 2, c, :], wo_sb[:, c, :], start=(c == 0), stop=(c == FC - 1))
                ins.then_inc(yo, 1)

            def ffn_scores(b):
                pe_.wait_ge(mnr, b + 1)
                mm(bank[6][0:1, 0:NE], mean_sb[:, b:b + 1], wr1_sb[:], start=True, stop=True).then_inc(sc, 1)

            def ffn_up(u, dst):
                g, c = u // FC, u % FC
                b = g // GB
                pe_.wait_ge(ld_ffn[b], 32)
                mm(dst[:], wffn_sb[b][:, P * c:P * (c + 1)], xT[:, G * g:G * (g + 1)], start=True, stop=True).then_inc(h2, 1)

            def ffn_down(t, bank_):
                g, i = t // TG, t % TG
                b = g // GB
                pe_.wait_ge(h2r, FC * (g + 1))
                dst = bank_[:, D * i:D * (i + 1)]
                for c in range(FC):
                    mm(dst, hid2[:, g % 2, c, P * i:P * (i + 1)], wffn_sb[b][:, FF + D * c:FF + D * (c + 1)],
                       start=(c == 0), stop=False)
                ins = mm(dst, ones[0:1, :], b2_sb[:, b, :], start=False, stop=True)
                if i == TG - 1:
                    ins.then_inc(y2, 1)

            pe_.wait_ge(consts, 5)
            pe_.wait_ge(narrowed, 3)
            pe_.wait_ge(krow, 4)
            pe_.wait_ge(cmb, 2 * NE * GB)
            def beside(work, i):
                shared_bank(work, i)
                if work == "turn":
                    pe_.wait_ge(xnr[2], TG * (i + 1))
                    turn(2, i, xn, bank[6])
                elif work == "values":
                    pe_.wait_ge(xtr[2], NG)
                    values(i, bank[6])
                elif work == "out_turn":
                    pe_.wait_ge(on, 2 * NH)
                    out_turn(i, bank[6])
                elif work == "out":
                    out_project(i, bank[6][:, 0:D])
                elif work == "ffn_turn":
                    pe_.wait_ge(xnr[3], TG * (i + 1))
                    turn(3, i, xn, bank[6])
                elif work == "ffn_scores":
                    ffn_scores(0)
                elif work == "ffn_up":
                    ffn_up(i, bank[6])
                elif work == "ffn_down":
                    ffn_down(i, bank[6])

            for r in range(4):
                project(0, r)
            for t in range(TB):
                if t < 2:
                    pe_.wait_ge(hd, 2 * NE * GB * HC)
                else:
                    pe_.wait_ge(vr, t - 1)
                values(t, bank[2 + t % 2])
                if t == 3:
                    for m in range(2):
                        max_chunk(0, m)
            for m in range(2, NC):
                max_chunk(0, m)
            max_turn(0)
            pe_.wait_ge(vr, TB)
            for n in range(NHD):
                pr = n // 2 + 1
                nxt = n % 2 == 0 and pr < NP
                for k in range(NS):
                    score(n, k)
                    if k >= LAG:
                        weigh(n, k - LAG)
                    elif n:
                        weigh(n - 1, NS + k - LAG)
                    if n + 1 < NHD:
                        for m in MAX_AT[k]:
                            max_chunk(n + 1, m)
                        if k == 8:
                            max_turn(n + 1)
                    if nxt and k in PROJ_AT:
                        project(pr, PROJ_AT[k])
                    work, i = BESIDE.get(n, {}).get(k, ("", 0))
                    if work:
                        beside(work, i)
            for k in range(NS - LAG, NS):
                weigh(NHD - 1, k)

            pe_.wait_ge(on, 2 * NHD)
            pe_.wait_ge(ex, NS * NHD)
            out_turn(TB, bank[TB % 2])
            for t in range(TB, NT):
                if t + 1 < NT:
                    if t > TB:
                        pe_.wait_ge(otr, t)
                    out_turn(t + 1, bank[(t + 1) % 2])
                out_project(t, bank[2 + t // TG % 2][:, D * (t % TG):D * (t % TG + 1)])
            pe_.wait_ge(otr, NT)
            for g in range(GB, NG):
                pe_.wait_ge(xnr[3], TG * (g + 1))
                turn(3, g, xn, bank[g % 2])
            pe_.wait_ge(res4, GB)
            ffn_scores(1)
            for g in range(GB, NG):
                for u in range(FC * g, FC * (g + 1)):
                    if u >= FC * GB + 2:
                        pe_.wait_ge(h2r, u - 1)
                    ffn_up(u, bank[4 + u % 2])
                for t in range(TG * g, TG * (g + 1)):
                    ffn_down(t, bank[2 + g % 2])


def kernel(L0_attn_x, L0_attn_Wg, L0_attn_bg, L0_attn_Wv, L0_attn_bv, L0_attn_Wd, L0_attn_bd, L0_ffn_norm_scale,
           L0_ffn_w_router, L0_ffn_w_up, L0_ffn_w_down, L1_attn_Wqkv, L1_attn_Wo, L1_ffn_Wr, L1_ffn_br, L1_ffn_W1,
           L1_ffn_b1, L1_ffn_W2, L1_ffn_b2):
    import numpy as np
    import concourse.bacc as bacc
    from concourse.bass_utils import run_bass_kernel_spmd

    def arr(a):
        return np.ascontiguousarray(np.asarray(a))

    wqkv = arr(L1_attn_Wqkv).reshape(NH // 2, 2, 3, HD, D)
    wqk = wqkv[:, :, 0:2].transpose(4, 0, 2, 1, 3).reshape(D, NH // 2, 2 * P)
    wv = wqkv[:, :, 2].transpose(3, 0, 1, 2).reshape(D, NH * HD)
    w_up = arr(L0_ffn_w_up).transpose(0, 2, 1)
    w_down = arr(L0_ffn_w_down).reshape(NE, D, HC, P).transpose(0, 3, 2, 1).reshape(NE, P, HC * D)
    w2 = arr(L1_ffn_W2).reshape(NE, FC, P, D).transpose(0, 2, 1, 3).reshape(NE, P, FC * D)
    b1 = arr(L1_ffn_b1).reshape(NE, FC, P).transpose(0, 2, 1)

    pos = np.arange(T, dtype=np.float32)[:, None]
    div = np.exp(np.arange(0, HD, 2, dtype=np.float32) * np.float32(-np.log(10000.0) / HD)).astype(np.float32)
    ang = (pos * div).astype(np.float32)
    table = np.stack([np.sin(ang), np.cos(ang)], axis=-1).reshape(T, HD).astype(np.float32)
    late = np.triu(np.full((P, P), -3.0e38, np.float32), 1)

    arrays = {
        "x": arr(L0_attn_x).reshape(B * T, D), "wg": arr(L0_attn_Wg), "wv0": arr(L0_attn_Wv), "wd": arr(L0_attn_Wd),
        "gate_bias": np.stack([arr(L0_attn_bg), arr(L0_attn_bv), arr(L0_attn_bd)], axis=1),
        "ns": arr(L0_ffn_norm_scale).reshape(D, 1), "wr0": arr(L0_ffn_w_router).T,
        "wexp": np.concatenate([w_up, w_down], axis=2), "wqk": wqk, "wv": wv,
        "wo": arr(L1_attn_Wo).T.reshape(FC, P, D).transpose(1, 0, 2), "wr1": arr(L1_ffn_Wr),
        "br1": arr(L1_ffn_br).reshape(1, NE),
        "wffn": np.concatenate([arr(L1_ffn_W1), w2, b1], axis=2), "b2": arr(L1_ffn_b2),
        "ident_d": np.eye(P, dtype=np.float32), "mask_d": late, "maskt_d": late.T,
        "pe_d": np.concatenate([table.T, table.T], axis=0),
        "iota_d": np.tile(np.arange(NE, dtype=np.float32), (P, 1)),
    }
    arrays = {k: np.ascontiguousarray(v) for k, v in arrays.items()}
    nc = bacc.Bacc("TRN2", target_bir_lowering=False, num_devices=1)
    args = [nc.dram_tensor(k, v.shape, mybir.dt.from_np(v.dtype), kind="ExternalInput").ap() for k, v in arrays.items()]
    args.append(nc.dram_tensor("out", (B * T, D), F32, kind="ExternalOutput").ap())
    mixed_layers_kernel(nc, *args)
    r = run_bass_kernel_spmd(nc, [arrays], core_ids=[0])
    return r.results[0]["out"].reshape(B, T, D)
```

```python
import math
from contextlib import ExitStack

import concourse.bass as bass
from concourse import mybir

F32 = mybir.dt.float32
F32R = mybir.dt.float32r
BF16 = mybir.dt.bfloat16
F16 = mybir.dt.float16
U32 = mybir.dt.uint32
ALU = mybir.AluOpType
ACT = mybir.ActivationFunctionType
AX_X = mybir.AxisListType.X

P = 128
D = 128
B, T = 2, 1024
NT = B * T // P
TB = T // P
G = 512
NG = B * T // G
GB = T // G
TG = G // P
EPS_LN, EPS_RMS = 1e-5, 1e-6
NE, HID = 8, 256
HC = HID // P
NH, HD = 8, 64
NP = B * NH // 2
NHD = B * NH
FF = 512
FC = FF // P
PT_RING = 7
P32_RING = 4
VONE = HD
VREST = HD + 1
VCOLS = 2 * HD + 2
P_SCALE = 16.0
V_SCALE = 1024.0
SCORE_BANKS = (2, 3, 7)
LAG = 4

STEPS = [(g, j, max(G * g, P * j), G * (g + 1) - max(G * g, P * j)) for g in range(GB) for j in range(TG * (g + 1))]
NS = len(STEPS)
HALF = (slice(0, HD), slice(HD, 2 * HD))
SHIFT_ROW = (HD, 0)
WITH_SHIFT = (slice(0, HD + 1), slice(0, 2 * HD))
POOL_STEPS = (0, 2, 4, 6, 8)
CHUNK_ORDER = [(4, 1), (2, 0), (3, 0), (4, 0), (5, 0), (6, 1), (6, 0), (7, 0), (7, 1), (1, 0), (5, 1), (0, 0)]
CHUNKS = [(i, c, min(G, P * (i + 1) - G * c)) for i, c in CHUNK_ORDER]
NC = len(CHUNKS)
TURN_AT = 7
MAX_AT = [(1, NC - TURN_AT + k) if k < TURN_AT else (2, k - TURN_AT) for k in range(NS)]
PROJ_AT = {0: 0, 1: 1, 3: 2, 4: 3}
ROUND_AT = {4: (0, 0), 5: (0, 1), 6: (1, 0), 7: (1, 1)}

BESIDE = {
    1: {0: ("turn", 2), 2: ("turn", 3), 4: ("values", 8), 6: ("values", 9)},
    3: {0: ("values", 10), 2: ("values", 11), 4: ("values", 12), 6: ("values", 13)},
    5: {0: ("values", 14), 2: ("values", 15)},
    8: {5: ("out_turn", 0), 6: ("out", 0)},
    9: {0: ("out_turn", 1), 1: ("out", 1), 2: ("out_turn", 2), 3: ("out", 2), 4: ("out_turn", 3), 5: ("out", 3),
        6: ("out_turn", 4), 7: ("out", 4)},
    10: {5: ("out_turn", 5), 6: ("out", 5)},
    11: {0: ("out_turn", 6), 1: ("out", 6), 2: ("out_turn", 7), 3: ("out", 7)},
    12: {5: ("ffn_turn", 0), 6: ("ffn_turn", 1), 7: ("ffn_scores", 0)},
    13: {4: ("ffn_up", 0), 5: ("ffn_up", 1), 6: ("ffn_up", 2), 7: ("ffn_up", 3)},
    14: {0: ("ffn_up", 4), 1: ("ffn_up", 5), 2: ("ffn_up", 6), 3: ("ffn_up", 7),
         4: ("ffn_down", 0), 5: ("ffn_down", 1), 6: ("ffn_down", 2), 7: ("ffn_down", 3)},
    15: {0: ("ffn_down", 4), 1: ("ffn_down", 5), 2: ("ffn_down", 6), 3: ("ffn_down", 7)},
}


def mixed_layers_kernel(nc, x, wg, wv0, wd, gate_bias, ns, wr0, wexp, wqk, wv, wo, wr1, br1, wffn, b2,
                        ident_d, mask_d, maskt_d, pe_d, iota_d, out):
    with ExitStack() as ctx:
        def sb(name, shape, dt=F32):
            return ctx.enter_context(nc.sbuf_tensor(name, shape, dt))

        def pb(name):
            return ctx.enter_context(nc.psum_tensor(name, [P, G], F32))

        def sem(name):
            return ctx.enter_context(nc.semaphore(name))

        xres = sb("xres", [P, NT, D])
        xn = sb("xn", [P, NT, D])
        xT = sb("xT", [P, B * T])
        stats = sb("stats", [P, NT, 6])
        mv = sb("mv", [P, NT, 2])
        rstd = sb("rstd", [P, NT])
        rtmp = sb("rtmp", [P, 4, NT])
        rrms = sb("rrms", [P, NT])
        euler = sb("euler", [P, NT])
        mhalf = sb("mhalf", [P, NT])
        ident = sb("ident", [P, P])
        identb = sb("identb", [P, P], BF16)
        maskb = sb("maskb", [P, P], BF16)
        masktb = sb("masktb", [P, P], BF16)
        pe = sb("pe", [P, T])
        iota = sb("iota", [P, NE])
        ones = sb("ones", [P, P])
        rec_bias = sb("rec_bias", [P, 3])
        ns_sb = sb("ns_sb", [P, 1])
        wr0_sb = sb("wr0_sb", [P, NE])
        wexp_sb = sb("wexp_sb", [P, 2, 2 * HID + HC * D])
        wqk_sb = sb("wqk_sb", [P, NH // 2, 2 * P])
        wv_sb = sb("wv_sb", [P, NH * HD])
        wo_sb = sb("wo_sb", [P, FC, D])
        wr1_sb = sb("wr1_sb", [P, NE])
        br1_sb = sb("br1_sb", [1, NE])
        shifts = sb("shifts", [P, 2, P], F32R)
        nmt = shifts[0:TB]
        scores, top = (shifts[:, i, :].bitcast(F32).rearrange("p (t e) -> p t e", t=NT) for i in range(2))
        topi = sb("topi", [P, NT, 8], U32)
        topf = sb("topf", [P, NT, 2])
        gap = sb("gap", [P, NT])
        egap = sb("egap", [P, NT])
        prob = sb("prob", [P, 2, NT])
        chosen = sb("chosen", [P, 2, NT, NE])
        cw = sb("cw", [P, NT, NE])
        vals = sb("vals", [P, NT, NH, VCOLS], F16)
        qk = sb("qk", [P, 2, T])
        qs = sb("qs", [P, 2, 2, T], F32R)
        kd = sb("kd", [P, 2, 2, T], F32R)
        qm = sb("qm", [P, 2, 2, T], F32R)
        kl = sb("kl", [P, 2, 2, T], F32R)
        p32 = sb("p32", [P, P32_RING, G])
        ph = sb("ph", [P, PT_RING, G], F16)
        pl = sb("pl", [P, PT_RING, G], F16)
        vnorm = sb("vnorm", [P, 3, FC])
        before = p32[:].rearrange("p a n -> p (a n)")
        w_rec = before[:, 0:3 * D].rearrange("p (w n) -> p w n", w=3)
        mask, maskt = before[:, 3 * D:3 * D + P], before[:, 3 * D + P:3 * D + 2 * P]
        wv2 = before[:, 2 * G:3 * G]
        att = sb("att", [P, NT, NH * HD])
        mx = sb("mx", [P, 2, TB, 2])
        mfin = sb("mfin", [P, 2, TB])
        rden = sb("rden", [P, 2, TG])
        attT = wexp_sb[:].rearrange("p a n -> p (a n)")[:, 0:2 * FC * P].rearrange("p (a c n) -> p a c n", a=2, c=FC)
        tok_sum = sb("tok_sum", [P, NG])
        mean_sb = sb("mean_sb", [P, B])
        sc1 = sb("sc1", [1, B, NE])
        top1 = sb("top1", [1, B, 8])
        top1i = sb("top1i", [1, B, 8], U32)

        wffn_sb = (vals[:, 0:TB].rearrange("p t h v -> p (t h v)").bitcast(F32)[:, 0:FF + FC * D + FC], qk[:].rearrange("p a n -> p (a n)")[:, 0:FF + FC * D + FC])
        b2_sb = chosen[0:1].rearrange("p r t e -> p (r t e)").rearrange("p (b d) -> p b d", b=B)
        early = att[:].rearrange("p t f -> p (t f)")
        sig = early[:, 0:2 * G].rearrange("p (a n) -> p a n", a=2)
        tnh = early[:, 2 * G:4 * G].rearrange("p (a n) -> p a n", a=2)
        dec = early[:, 4 * G:6 * G].rearrange("p (a n) -> p a n", a=2)
        scan_in = early[:, 6 * G:8 * G].rearrange("p (a n) -> p a n", a=2)
        hT = early[:, 8 * G:12 * G]
        silu = early[:, 0:2 * G].rearrange("p (a n) -> p a n", a=2)
        hid = early[:, 2 * G:6 * G].rearrange("p (a n) -> p a n", a=4)
        xrms = early[:, 12 * G:16 * G].rearrange("p (t d) -> p t d", t=NT)
        hid2 = early[:, 0:8 * G].rearrange("p (a c n) -> p a c n", a=2, c=FC)

        xhi, xlo = qs[:, 0].rearrange("p a n -> p (a n)"), qs[:, 1].rearrange("p a n -> p (a n)")
        wsp = kd[:, 0].rearrange("p a n -> p (a n)").rearrange("p (s r n) -> p s r n", s=2, r=2)

        bank = [pb(f"bank{i}") for i in range(8)]

        ld_x, ld_rec, ld_w = [sem("ld_x0"), sem("ld_x1")], sem("ld_rec"), sem("ld_w")
        ld_up, ld_down = [sem("ld_up0"), sem("ld_up1")], [sem("ld_down0"), sem("ld_down1")]
        ld_ffn, ld_ffn2 = [sem("ld_ffn0"), sem("ld_ffn1")], [sem("ld_ffn20"), sem("ld_ffn21")]
        consts, narrowed = sem("consts"), sem("narrowed")
        bn = [sem(f"bn{s}") for s in range(4)]
        mvr = [sem(f"mv{s}") for s in range(4)]
        ve, rrmsr = sem("ve"), sem("rrmsr")
        rs = [sem(f"rstd{s}") for s in range(4)]
        xnr = [sem(f"xn{s}") for s in range(4)]
        tr = [sem(f"tr{s}") for s in range(4)]
        xtr = [sem(f"xt{s}") for s in range(4)]
        proj0, gates = sem("proj0"), sem("gates")
        dvs, krow = sem("dvs"), sem("krow")
        scanned, back, res1 = sem("scanned"), sem("back"), sem("res1")
        wsplit, xrest = sem("wsplit"), sem("xrest")
        rms, routed, skipped = sem("rms"), sem("routed"), sem("skipped")
        rout, gapr, egr, cwr = sem("rout"), sem("gapr"), sem("egr"), sem("cwr")
        up, si, hd, dn, cmb = sem("up"), sem("si"), sem("hd"), sem("dn"), sem("cmb")
        vp, vr = sem("vp"), sem("vr")
        pj, qkd, hi, qlo, klo, dup = (sem(s) for s in ("pj", "qkd", "hi", "qlo", "klo", "dup"))
        mp, mr, mf, mt, nm, mrow = sem("mp"), sem("mr"), sem("mf"), sem("mt"), sem("nm"), sem("mrow")
        st, ex, pv, den, on = sem("st"), sem("ex"), sem("pv"), sem("den"), sem("on")
        pld, plp, vhr = sem("pld"), sem("plp"), sem("vhr")
        wsq, vn, vnp, vnr, vdg, vbc, wvr, wor = (sem(n) for n in ("wsq", "vn", "vnp", "vnr", "vdg", "vbc", "wvr", "wor"))
        ot, otr, yo, res3 = sem("ot"), sem("otr"), sem("yo"), sem("res3")
        mnr, sc, idx = sem("mnr"), sem("sc"), sem("idx")
        h2, h2r, y2, res4, stored = sem("h2"), sem("h2r"), sem("y2"), sem("res4"), sem("stored")

        x_v = x.rearrange("(t p) d -> p t d", p=P)
        out_v = out.rearrange("(t p) d -> p t d", p=P)
        loads_rec = [(ident[:], ident_d), (w_rec[:, 0, :], wg), (w_rec[:, 1, :], wv0), (w_rec[:, 2, :], wd),
                     (rec_bias[:], gate_bias)]
        loads = [(ns_sb[:], ns), (wr0_sb[:], wr0), (iota[:], iota_d), (mask[:], mask_d), (maskt[:], maskt_d),
                 (pe[:], pe_d), (wqk_sb[:], wqk), (wv_sb[:], wv), (wo_sb[:], wo), (wr1_sb[:], wr1), (br1_sb[:], br1)]
        ALL_REC, ALL_W = 16 * len(loads_rec), 16 * len(loads)

        block = ctx.enter_context(nc.Block())

        @block.sync
        def _(sp):
            for g in range(NG):
                sp.dma_start(xres[:, TG * g:TG * (g + 1), :], x_v[:, TG * g:TG * (g + 1), :]).then_inc(ld_x[g // GB], 16)
            for w in range(B * NE):
                if w >= 2:
                    sp.wait_ge(wsplit, 2 * (w - 1))
                sp.dma_start(wexp_sb[:, w % 2, 0:2 * HID], wexp[w % NE, :, 0:2 * HID]).then_inc(ld_up[w % 2], 16)
                if w >= 2:
                    sp.wait_ge(dn, (w - 1) * GB)
                sp.dma_start(wexp_sb[:, w % 2, 2 * HID:], wexp[w % NE, :, 2 * HID:]).then_inc(ld_down[w % 2], 16)

            def copies(pr):
                for a in range(2):
                    sp.wait_ge(hi, 4 * pr + 2 * a + 2)
                    own, other = HALF[a], HALF[1 - a]
                    sp.dma_start(qm[own, pr % 2, a, :].bitcast(F32), qs[own, pr % 2, a, :].bitcast(F32)).then_inc(dup, 16)
                    sp.dma_start(kd[other, pr % 2, a, :].bitcast(F32), kd[own, pr % 2, a, :].bitcast(F32)).then_inc(dup, 16)

            def chosen_expert(b):
                sp.wait_ge(idx, 2 * (b + 1))
                e = sp.value_load(top1i[0:1, b, 0:1], min_val=0, max_val=NE - 1)
                first, second = slice(0, FF + FC), slice(FF + FC, FF + FC + FC * D)
                sp.dma_start(wffn_sb[b][:, first], wffn[bass.ds(e, 1), :, first].rearrange("a p n -> (a p) n")).then_inc(ld_ffn[b], 16)
                sp.dma_start(wffn_sb[b][:, second], wffn[bass.ds(e, 1), :, second].rearrange("a p n -> (a p) n")).then_inc(ld_ffn2[b], 16)
                sp.dma_start(b2_sb[:, b, :], b2[bass.ds(e, 1), :]).then_inc(ld_ffn2[b], 16)

            def store(g):
                sp.wait_ge(res4, g + 1)
                sp.dma_start(out_v[:, TG * g:TG * (g + 1), :], xres[:, TG * g:TG * (g + 1), :]).then_inc(stored, 16)

            copies(0)
            for n in range(NHD):
                sp.wait_ge(nm, n + 1)
                a, pr = n % 2, n // 2
                sp.dma_start(qm[SHIFT_ROW[a]:SHIFT_ROW[a] + 1, pr % 2, a, :].bitcast(F32), nmt[:, a, :].bitcast(F32)).then_inc(mrow, 16)
                if n % 2 and pr + 1 < NP:
                    copies(pr + 1)
                if n == 13:
                    chosen_expert(0)
            store(0)
            store(1)
            chosen_expert(1)
            store(2)
            store(3)
            sp.wait_ge(stored, 16 * NG)

        def probability_rest(engine, eng, n, k, done):
            u, w = NS * n + k, STEPS[k][3]
            eng.wait_ge(ex, u + 1)
            if u >= PT_RING:
                eng.wait_ge(pv, u - PT_RING + 1)
            engine.tensor_tensor(pl[:, u % PT_RING, 0:w], p32[:, u % P32_RING, 0:w], ph[:, u % PT_RING, 0:w],
                                 ALU.subtract).then_inc(done, 1)

        def rests(n, k):
            by_pool = n * len(POOL_STEPS) + sum(s <= k for s in POOL_STEPS)
            return by_pool, NS * n + k + 1 - by_pool

        @block.gpsimd
        def _(pool):
            nc.gpsimd.memset(mhalf[:], -0.5).then_inc(consts, 1)
            nc.gpsimd.memset(ones[:], 1.0).then_inc(consts, 1)
            nc.gpsimd.memset(vals[:, :, :, VONE:VONE + 1], 1.0).then_inc(consts, 1)
            nc.gpsimd.memset(mx[:], -3.0e38).then_inc(consts, 1)
            nc.gpsimd.memset(euler[:], math.e).then_inc(consts, 1)
            pool.wait_ge(consts, 5)
            def inverse_deviation(s, b):
                t = slice(TB * b, TB * (b + 1))
                pool.wait_ge(mvr[s], TB * (b + 1))
                nc.gpsimd.tensor_scalar_add(rtmp[:, 0, t], mv[:, t, 1], EPS_LN).then_inc(ve, 1)
                veq[0] += 1
                pool.wait_ge(ve, veq[0])
                nc.gpsimd.tensor_tensor(rstd[:, t], rtmp[:, 0, t], mhalf[:, t], ALU.pow).then_inc(rs[s], 1)
                pool.wait_ge(rs[s], b + 1)

            veq = [0]

            def inverse_rms(b):
                t = slice(TB * b, TB * (b + 1))
                pool.wait_ge(mvr[1], TB * (b + 1))
                nc.gpsimd.tensor_scalar(rtmp[:, 1, t], mv[:, t, 1], 1.0 + EPS_RMS, EPS_RMS * EPS_LN, ALU.mult,
                                        ALU.add).then_inc(ve, 1)
                veq[0] += 1
                pool.wait_ge(ve, veq[0])
                nc.gpsimd.tensor_tensor(rrms[:, t], rtmp[:, 1, t], mhalf[:, t], ALU.pow).then_inc(rrmsr, 1)
                pool.wait_ge(rrmsr, b + 1)

            def second_weight(b):
                t = slice(TB * b, TB * (b + 1))
                pool.wait_ge(gapr, b + 1)
                nc.gpsimd.tensor_tensor(egap[:, t], euler[:, t], gap[:, t], ALU.pow).then_inc(egr, 1)
                pool.wait_ge(egr, b + 1)

            def value_norms():
                pool.wait_ge(ld_w, ALL_W)
                nc.gpsimd.tensor_tensor(wv2[:], wv_sb[:], wv_sb[:], ALU.mult).then_inc(wsq, 1)

            def value_scales():
                pool.wait_ge(vnp, 1)
                nc.gpsimd.tensor_tensor(vnorm[:, 1, :], vnorm[:, 0, :], mhalf[:, 0:FC], ALU.pow).then_inc(vnr, 1)
                pool.wait_ge(vnr, 1)

            def split_weights(w):
                pool.wait_ge(ld_up[w % 2], 16 * (w // 2 + 1))
                if w >= 2:
                    pool.wait_ge(up, GB * HC * (w - 1))
                whole = wexp_sb[:, w % 2, 0:2 * HID]
                nc.gpsimd.tensor_copy(wsp[:, w % 2, 0, :], whole).then_inc(wsplit, 1)
                pool.wait_ge(wsplit, 2 * w + 1)
                nc.gpsimd.tensor_tensor(wsp[:, w % 2, 1, :], whole, wsp[:, w % 2, 0, :].bitcast(F32),
                                        ALU.subtract).then_inc(wsplit, 1)

            def shift_rows():
                for i, (dst, value) in enumerate(((qm[0:HD, :, 1, :], 0.0), (kl[0:HD, :, 1, :], 0.0), (kl[0:1, :, 1, :], 1.0),
                                                  (kl[HD:HD + 1, :, 0, :], 1.0))):
                    nc.gpsimd.memset(dst.bitcast(F32), value).then_inc(krow, 1)
                    pool.wait_ge(krow, i + 1)

            inverse_deviation(0, 0)
            inverse_deviation(0, 1)
            split_weights(0)
            split_weights(1)
            shift_rows()
            value_norms()
            inverse_rms(0)
            inverse_deviation(1, 0)
            second_weight(0)
            split_weights(2)
            inverse_rms(1)
            inverse_deviation(1, 1)
            for w in range(3, 6):
                split_weights(w)
            second_weight(1)
            split_weights(6)
            value_scales()
            for w in range(7, NE + 3):
                split_weights(w)
            inverse_deviation(2, 0)
            for w in range(NE + 3, 2 * NE):
                split_weights(w)

            def key_rest(pr, a):
                pool.wait_ge(hi, 4 * pr + 2 * a + 2)
                own = HALF[a]
                nc.gpsimd.tensor_tensor(kl[own, pr % 2, a, :], qk[own, 1, :], kd[own, pr % 2, a, :].bitcast(F32),
                                        ALU.subtract).then_inc(klo, 1)
                pool.wait_ge(klo, 2 * pr + a + 1)

            key_rest(0, 0)
            key_rest(0, 1)
            inverse_deviation(2, 1)
            for n in range(NHD):
                for i, k in enumerate(POOL_STEPS):
                    probability_rest(nc.gpsimd, pool, n, k, plp)
                    pool.wait_ge(plp, rests(n, k)[0])
                    if n % 2 and i == 2 and (n + 1) // 2 < NP:
                        key_rest((n + 1) // 2, 1)
                if n % 2 == 0 and n // 2 + 1 < NP:
                    key_rest(n // 2 + 1, 0)
                if n == 11:
                    inverse_deviation(3, 0)
            inverse_deviation(3, 1)

        @block.scalar
        def _(act):
            for dst, src in loads_rec:
                act.dma_start(dst, src).then_inc(ld_rec, 16)
            for dst, src in loads:
                act.dma_start(dst, src).then_inc(ld_w, 16)

            def turn(s, g, src, scale=1.0):
                act.wait_ge(tr[s], g + 1)
                nc.scalar.activation(xT[:, G * g:G * (g + 1)], src[:], ACT.Copy, scale=scale).then_inc(xtr[s], 1)

            def scaled_turn(g):
                act.wait_ge(tr[1], g + 1)
                nc.scalar.activation(xhi[:, G * g:G * (g + 1)], bank[g % 2][:], ACT.Copy, scale=ns_sb[:, 0:1])
                turn(1, g, bank[g % 2], ns_sb[:, 0:1])

            def recurrent_gates(g):
                act.wait_ge(proj0, g + 1)
                if g >= 2:
                    act.wait_ge(scanned, g - 1)
                for w, (dst, func) in enumerate(((sig, ACT.Sigmoid), (tnh, ACT.Tanh), (dec, ACT.Sigmoid))):
                    nc.scalar.activation(dst[:, g % 2, :], bank[2 + 3 * (g % 2) + w][:], func,
                                         bias=rec_bias[:, w:w + 1]).then_inc(gates, 1)

            def expert(w):
                for u in range(w * GB * HC, (w + 1) * GB * HC):
                    act.wait_ge(up, u + 1)
                    if u >= 2:
                        act.wait_ge(hd, u - 1)
                    nc.scalar.activation(silu[:, u % 2, :], bank[2 + 2 * (u % 2)][:], ACT.Silu).then_inc(si, 1)

            def values(t, src):
                act.wait_ge(vp, t + 1)
                nc.scalar.copy(vals[:, t, :, 0:HD], src[:].rearrange("p (h d) -> p h d", h=NH)).then_inc(vhr, 1)

            def out_turn(t, src):
                act.wait_ge(ot, t + 1)
                if t >= 2:
                    act.wait_ge(yo, t - 1)
                nc.scalar.copy(attT[:, t % 2].rearrange("p c n -> p (c n)"), src[:]).then_inc(otr, 1)

            def ffn_turn(g, src):
                act.wait_ge(tr[3], g + 1)
                nc.scalar.activation(xT[:, G * g:G * (g + 1)], src[:], ACT.Copy,
                                     accum_out=tok_sum[:, g:g + 1]).then_inc(xtr[3], 1)

            def ffn_up(u, src):
                g, c = u // FC, u % FC
                b = g // GB
                act.wait_ge(ld_ffn[b], 16)
                act.wait_ge(h2, u + 1)
                if g >= 2:
                    act.wait_ge(y2, g - 1)
                nc.scalar.activation(hid2[:, g % 2, c, :], src[:], ACT.Relu,
                                     bias=wffn_sb[b][:, FF + c:FF + c + 1]).then_inc(h2r, 1)

            act.wait_ge(ld_rec, ALL_REC)
            turn(0, 0, bank[0])
            turn(0, 1, bank[1])
            recurrent_gates(0)
            recurrent_gates(1)
            turn(0, 2, bank[0])
            turn(0, 3, bank[1])
            recurrent_gates(2)
            recurrent_gates(3)
            act.wait_ge(ld_w, ALL_W)
            scaled_turn(0)
            scaled_turn(1)
            for w in range(3):
                expert(w)
            scaled_turn(2)
            scaled_turn(3)
            nc.scalar.copy(identb[:], ident[:]).then_inc(narrowed, 1)
            nc.scalar.copy(maskb[:], mask[:]).then_inc(narrowed, 1)
            nc.scalar.copy(masktb[:], maskt[:]).then_inc(narrowed, 1)
            for w in range(3, NE + 3):
                expert(w)
            turn(2, 0, bank[0])
            turn(2, 1, bank[1])
            for w in range(NE + 3, 2 * NE):
                expert(w)

            def round_half(pr, a, r):
                act.wait_ge(qkd, 4 * pr + 2 * r + 2)
                if pr:
                    act.wait_ge(st, NS * 2 * (pr - 1) + 1)
                dst = (qs, kd)[r]
                nc.scalar.copy(dst[HALF[a], pr % 2, a, :], qk[HALF[a], r, :]).then_inc(hi, 1)

            for a in range(2):
                for r in range(2):
                    round_half(0, a, r)
            for t in range(TB):
                values(t, bank[2 + t % 4])
            for n in range(NHD):
                for k, (g, j, q0, w) in enumerate(STEPS):
                    u = NS * n + k
                    act.wait_ge(st, u + 1)
                    if u >= PT_RING:
                        act.wait_ge(pv, u - PT_RING + 1)
                    if u >= P32_RING:
                        by_pool, by_vector = rests(*divmod(u - P32_RING, NS))
                        if (u - P32_RING) % NS in POOL_STEPS:
                            act.wait_ge(plp, by_pool)
                        else:
                            act.wait_ge(pld, by_vector)
                    nc.scalar.activation(ph[:, u % PT_RING, 0:w], bank[SCORE_BANKS[u % 3]][:, 0:w], ACT.Exp,
                                         scale=HD ** -0.5)
                    nc.scalar.activation(p32[:, u % P32_RING, 0:w], bank[SCORE_BANKS[u % 3]][:, 0:w], ACT.Exp,
                                         scale=HD ** -0.5).then_inc(ex, 1)
                    if n % 2 == 0 and n // 2 + 1 < NP and k in ROUND_AT:
                        round_half(n // 2 + 1, *ROUND_AT[k])
                    work, i = BESIDE.get(n, {}).get(k, ("", 0))
                    if work == "turn":
                        turn(2, i, bank[6])
                    elif work == "values":
                        values(i, bank[6])
                    elif work == "out_turn":
                        out_turn(i, bank[6])
                    elif work == "ffn_turn":
                        ffn_turn(i, bank[6])
                    elif work == "ffn_up":
                        ffn_up(i, bank[6])
            for t in range(TB, NT):
                out_turn(t, bank[t % 2])
            for g in range(GB, NG):
                ffn_turn(g, bank[g % 2])
            for u in range(FC * GB, FC * NG):
                ffn_up(u, bank[4 + u % 2])

        @block.vector
        def _(dve):
            links = [0]

            def link(ins):
                links[0] += 1
                ins.then_inc(dvs, 1)
                dve.wait_ge(dvs, links[0])

            def tile_stats(s, tiles):
                for t in tiles:
                    nc.vector.bn_stats(stats[:, t, :], xres[:, t, :]).then_inc(bn[s], 1)

            def tile_moments(s, tiles):
                dve.wait_ge(bn[s], tiles.stop)
                for t in tiles:
                    nc.vector.bn_aggr(mv[:, t, :], stats[:, t, :]).then_inc(mvr[s], 1)

            def norm_stats(s, b):
                tile_stats(s, range(TB * b, TB * (b + 1)))
                tile_moments(s, range(TB * b, TB * (b + 1)))

            def norm_apply(s, b):
                dve.wait_ge(rs[s], b + 1)
                dve.wait_ge(mvr[s], TB * (b + 1))
                for t in range(TB * b, TB * (b + 1)):
                    nc.vector.tensor_scalar(xn[:, t, :], xres[:, t, :], mv[:, t, 0:1], rstd[:, t:t + 1],
                                            ALU.subtract, ALU.mult).then_inc(xnr[s], 1)

            def residual(g, src, ready, value, done):
                dve.wait_ge(ready, value)
                tg = slice(TG * g, TG * (g + 1))
                nc.vector.tensor_tensor(xres[:, tg, :], xres[:, tg, :], src[:].rearrange("p (t d) -> p t d", t=TG),
                                        ALU.add).then_inc(done, 1)

            def scan(g):
                dve.wait_ge(gates, 3 * (g + 1))
                if g >= 2:
                    dve.wait_ge(scanned, g - 1)
                nc.vector.tensor_tensor(scan_in[:, g % 2, :], sig[:, g % 2, :], tnh[:, g % 2, :], ALU.mult).then_inc(dvs, 1)
                nc.vector.tensor_scalar(dec[:, g % 2, :], dec[:, g % 2, :], 0.998, 0.001, ALU.mult, ALU.add).then_inc(dvs, 1)
                links[0] += 2
                dve.wait_ge(dvs, links[0])
                if g % GB:
                    dve.wait_ge(scanned, g)
                first = 0.0 if g % GB == 0 else hT[:, G * g - 1:G * g]
                nc.vector.tensor_tensor_scan(hT[:, G * g:G * (g + 1)], dec[:, g % 2, :], scan_in[:, g % 2, :], first,
                                             ALU.mult, ALU.add).then_inc(scanned, 1)

            def rms_apply(b):
                dve.wait_ge(rrmsr, b + 1)
                for t in range(TB * b, TB * (b + 1)):
                    nc.vector.tensor_scalar(xrms[:, t, :], xres[:, t, :], mv[:, t, 0:1], rrms[:, t:t + 1],
                                            ALU.subtract, ALU.mult).then_inc(rms, 1)

            def skip(b):
                norm_apply(1, b)
                dve.wait_ge(xnr[1], TB * (b + 1))
                dve.wait_ge(rms, TB * (b + 1))
                tb = slice(TB * b, TB * (b + 1))
                nc.vector.tensor_tensor(xres[:, tb, :], xres[:, tb, :], xn[:, tb, :], ALU.add).then_inc(skipped, 1)

            def token_rest(g):
                dve.wait_ge(xtr[1], g + 1)
                tok = slice(G * g, G * (g + 1))
                nc.vector.tensor_tensor(xlo[:, tok], xT[:, tok], xhi[:, tok].bitcast(F32), ALU.subtract).then_inc(xrest, 1)

            def route(b):
                tb = slice(TB * b, TB * (b + 1))
                dve.wait_ge(rout, b + 1)
                nc.vector.tensor_copy(scores[:, tb, :], bank[0][:, 0:TB * NE].rearrange("p (t e) -> p t e", t=TB)).then_inc(routed, 1)
                dve.wait_ge(routed, b + 1)
                for t in range(TB * b, TB * (b + 1)):
                    ins = nc.vector.max(top[:, t, :], scores[:, t, :])
                link(ins)
                nc.vector.tensor_tensor(gap[:, tb], top[:, tb, 1], top[:, tb, 0], ALU.subtract).then_inc(gapr, 1)
                for t in range(TB * b, TB * (b + 1)):
                    ins = nc.vector.max_index(topi[:, t, :], top[:, t, :], scores[:, t, :])
                link(ins)
                link(nc.vector.tensor_copy(topf[:, tb, :], topi[:, tb, 0:2]))
                for r in range(2):
                    ins = nc.vector.tensor_tensor(chosen[:, r, tb], iota[:].unsqueeze(1).to_broadcast([P, TB, NE]),
                                                  topf[:, tb, r:r + 1].to_broadcast([P, TB, NE]), ALU.is_equal)
                dve.wait_ge(egr, b + 1)
                link(nc.vector.tensor_scalar(prob[:, 1, tb], egap[:, tb], 1.0, None, ALU.add))
                link(nc.vector.reciprocal(prob[:, 0, tb], prob[:, 1, tb]))
                link(nc.vector.tensor_tensor(prob[:, 1, tb], prob[:, 0, tb], egap[:, tb], ALU.mult))
                for r in range(2):
                    ins = nc.vector.tensor_tensor(chosen[:, r, tb], chosen[:, r, tb],
                                                  prob[:, r, tb].unsqueeze(2).to_broadcast([P, TB, NE]), ALU.mult)
                link(ins)
                nc.vector.tensor_tensor(cw[:, tb], chosen[:, 0, tb], chosen[:, 1, tb], ALU.add).then_inc(cwr, 1)

            def combine(v):
                w, g = v // GB, v // (NE * GB) * GB + v % GB
                dve.wait_ge(dn, v + 1)
                if w % NE == 0:
                    dve.wait_ge(cwr, w // NE + 1)
                    dve.wait_ge(skipped, w // NE + 1)
                else:
                    dve.wait_ge(cmb, v - GB + 1)
                for i in range(TG):
                    t = TG * g + i
                    ins = nc.vector.scalar_tensor_tensor(xres[:, t, :], bank[6 + v % 2][:, D * i:D * (i + 1)],
                                                         cw[:, t, w % NE:w % NE + 1], xres[:, t, :], ALU.mult, ALU.add)
                ins.then_inc(cmb, 1)

            def expert(w):
                for v in range(w * GB, (w + 1) * GB):
                    for u in range(v * HC, (v + 1) * HC):
                        dve.wait_ge(si, u + 1)
                        if u >= 4:
                            dve.wait_ge(dn, u // HC - 1)
                        nc.vector.tensor_tensor(hid[:, u % 4, :], bank[3 + 2 * (u % 2)][:], silu[:, u % 2, :],
                                                ALU.mult).then_inc(hd, 1)
                    if v:
                        combine(v - 1)

            for b in range(B):
                dve.wait_ge(ld_x[b], 16 * GB)
                norm_stats(0, b)
                if b:
                    norm_apply(0, b - 1)
            norm_apply(0, B - 1)
            scan(0)
            scan(1)
            for g in range(GB):
                residual(g, bank[g % 2], back, g + 1, res1)
            dve.wait_ge(res1, GB)
            norm_stats(1, 0)
            scan(2)
            scan(3)

            rms_apply(0)
            for g in range(GB, NG):
                residual(g, bank[2 + g % 2], back, g + 1, res1)
            token_rest(0)
            token_rest(1)
            skip(0)
            route(0)
            expert(0)
            dve.wait_ge(res1, NG)
            norm_stats(1, 1)
            expert(1)
            rms_apply(1)
            expert(2)
            skip(1)
            expert(3)
            token_rest(2)
            token_rest(3)
            expert(4)
            route(1)
            for w in range(5, NE + 1):
                expert(w)
                if w == 5:
                    dve.wait_ge(consts, 5)
                    dve.wait_ge(ld_w, ALL_W)
                    dve.wait_ge(vn, 1)
                    nc.vector.tensor_scalar(vnorm[:, 0, :], bank[1][:, 0:FC], D / V_SCALE ** 2, 1e-30, ALU.mult,
                                            ALU.add).then_inc(vnp, 1)
                elif w == 6:
                    dve.wait_ge(vnr, 1)
                    for c in range(FC):
                        ins = nc.vector.tensor_scalar(wv2[:, P * c:P * (c + 1)], ident[:], vnorm[:, 1, c:c + 1], None, ALU.mult)
                    ins.then_inc(vdg, 1)
                    link(nc.vector.reciprocal(vnorm[:, 2, :], vnorm[:, 1, :]))
                    for c in range(FC):
                        ins = nc.vector.tensor_scalar(wo_sb[:, c, :], wo_sb[:, c, :], vnorm[:, 2, c:c + 1], None, ALU.mult)
                    ins.then_inc(wor, 1)
                elif w == 7:
                    dve.wait_ge(vbc, 1)
                    nc.vector.tensor_tensor(wv_sb[:], wv_sb[:], bank[1][:], ALU.mult).then_inc(wvr, 1)
            dve.wait_ge(cmb, NE * GB)
            norm_stats(2, 0)
            expert(NE + 1)
            norm_apply(2, 0)
            for w in range(NE + 2, 2 * NE):
                expert(w)
            combine(2 * NE * GB - 1)

            def evacuate(pr, r):
                dve.wait_ge(pj, 4 * pr + r + 1)
                if pr:
                    dve.wait_ge(hi, 4 * pr)
                    dve.wait_ge(qlo, 2 * pr)
                    dve.wait_ge(klo, 2 * pr)
                half = slice(G * (r % 2), G * (r % 2 + 1))
                nc.vector.tensor_tensor(qk[:, r // 2, half], bank[6 if pr else 2 + r][:], pe[:, half], ALU.add).then_inc(qkd, 1)

            def query_rest(pr, a):
                dve.wait_ge(hi, 4 * pr + 2 * a + 1)
                own, other = HALF[a], HALF[1 - a]
                nc.vector.tensor_tensor(qs[other, pr % 2, a, :], qk[own, 0, :], qs[own, pr % 2, a, :].bitcast(F32),
                                        ALU.subtract).then_inc(qlo, 1)

            def max_chunk(n, m):
                i, c, w = CHUNKS[m]
                dve.wait_ge(mp, NC * n + m + 1)
                nc.vector.tensor_reduce(mx[:, n % 2, i, c:c + 1], bank[(NC * n + m) % 2][:, 0:w], AX_X,
                                        ALU.max).then_inc(mr, 1)

            def max_final(n):
                dve.wait_ge(mr, NC * (n + 1))
                nc.vector.tensor_reduce(mfin[:, n % 2, :], mx[:, n % 2], AX_X, ALU.max).then_inc(mf, 1)

            def max_row(n):
                dve.wait_ge(mt, n + 1)
                if n >= 2:
                    dve.wait_ge(mrow, 16 * (n - 1))
                nc.vector.tensor_scalar(nmt[:, n % 2, :], bank[6][0:TB, 0:P], -1.0,
                                        HD ** 0.5 * math.log(P_SCALE), ALU.mult, ALU.add).then_inc(nm, 1)

            def normalise(n, g):
                b, h = n // NH, n % NH
                dve.wait_ge(pv, NS * n + (TG if g == 0 else NS))
                o = bank[4 + g][:, 0:TG * (HD + 1)].rearrange("p (t d) -> p t d", t=TG)
                nc.vector.reciprocal(rden[:, g, :], o[:, :, HD]).then_inc(den, 1)
                dve.wait_ge(den, 2 * n + g + 1)
                nc.vector.tensor_tensor(att[:, TB * b + TG * g:TB * b + TG * (g + 1), HD * h:HD * (h + 1)], o[:, :, 0:HD],
                                        rden[:, g, :].unsqueeze(2).to_broadcast([P, TG, HD]), ALU.mult).then_inc(on, 1)

            def out_add(t, src):
                dve.wait_ge(yo, t + 1)
                nc.vector.tensor_tensor(xres[:, t, :], xres[:, t, :], src, ALU.add).then_inc(res3, 1)

            def best_expert(b):
                dve.wait_ge(xtr[3], GB * (b + 1))
                link(nc.vector.tensor_tensor(mean_sb[:, b:b + 1], tok_sum[:, GB * b:GB * b + 1],
                                             tok_sum[:, GB * b + 1:GB * b + 2], ALU.add))
                nc.vector.tensor_scalar(mean_sb[:, b:b + 1], mean_sb[:, b:b + 1], 1.0 / T, None, ALU.mult).then_inc(mnr, 1)
                dve.wait_ge(sc, b + 1)
                link(nc.vector.tensor_tensor(sc1[:, b, :], bank[6][0:1, 0:NE], br1_sb[:], ALU.add))
                nc.vector.max(top1[:, b, :], sc1[:, b, :]).then_inc(idx, 1)
                dve.wait_ge(idx, 2 * b + 1)
                nc.vector.max_index(top1i[:, b, :], top1[:, b, :], sc1[:, b, :]).then_inc(idx, 1)

            def value_rest(t, src):
                dve.wait_ge(vhr, t + 1)
                nc.vector.tensor_tensor(vals[:, t, :, VREST:VREST + HD], src[:].rearrange("p (h d) -> p h d", h=NH),
                                        vals[:, t, :, 0:HD], ALU.subtract).then_inc(vr, 1)

            for r in range(4):
                evacuate(0, r)
            query_rest(0, 0)
            query_rest(0, 1)
            for t in range(TB):
                value_rest(t, bank[2 + t % 4])
                if t >= 3:
                    max_chunk(0, 2 * (t - 3))
                    max_chunk(0, 2 * (t - 3) + 1)
            for m in range(10, NC):
                max_chunk(0, m)
            max_final(0)
            max_row(0)
            for m in range(NC - TURN_AT):
                max_chunk(1, m)
            dve.wait_ge(cmb, 2 * NE * GB)
            norm_stats(2, 1)
            for n in range(NHD):
                pr = n // 2 + 1
                nxt = n % 2 == 0 and pr < NP
                for k in range(NS):
                    ahead, m = MAX_AT[k]
                    if n + ahead < NHD and k < TURN_AT:
                        max_chunk(n + ahead, m)
                    if n + 1 < NHD:
                        if k == TURN_AT:
                            max_final(n + 1)
                        if k == TURN_AT + 1:
                            max_row(n + 1)
                    if n + ahead < NHD and k >= TURN_AT:
                        max_chunk(n + ahead, m)
                    if nxt and k in PROJ_AT:
                        evacuate(pr, PROJ_AT[k])
                    if k and k - 1 not in POOL_STEPS:
                        probability_rest(nc.vector, dve, n, k - 1, pld)
                    elif k == 0 and n and NS - 1 not in POOL_STEPS:
                        probability_rest(nc.vector, dve, n - 1, NS - 1, pld)
                    if nxt and k in (9, 11):
                        query_rest(pr, (k - 9) // 2)
                    if k == TG - 1 + LAG:
                        normalise(n, 0)
                    if k == LAG - 1 and n:
                        normalise(n - 1, 1)
                    work, i = BESIDE.get(n, {}).get(k, ("", 0))
                    if work == "values":
                        value_rest(i, bank[6])
                    elif work == "out":
                        out_add(i, bank[6][:, 0:D])
                    elif work == "ffn_scores":
                        best_expert(i)
                    elif work == "ffn_down" and i % TG == TG - 1:
                        residual(i // TG, bank[6], y2, i // TG + 1, res4)
                    if (n, k) == (0, 10):
                        norm_apply(2, 1)
                    if (n, k) == (11, 8):
                        dve.wait_ge(res3, TB)
                        norm_stats(3, 0)
                    if (n, k) == (12, 3):
                        norm_apply(3, 0)
            if NS - 1 not in POOL_STEPS:
                probability_rest(nc.vector, dve, NHD - 1, NS - 1, pld)
            normalise(NHD - 1, 1)

            for g in range(GB, NG):
                residual(g, bank[2 + g % 2], yo, TG * (g + 1), res3)
                dve.wait_ge(res3, TB + g - GB + 1)
                tile_stats(3, range(TG * g, TG * (g + 1)))
            tile_moments(3, range(TB, NT))
            norm_apply(3, 1)
            best_expert(1)
            for g in range(GB, NG):
                residual(g, bank[2 + g % 2], y2, g + 1, res4)

        @block.tensor
        def _(pe_):
            mm = nc.tensor.matmul

            def turn(s, g, src, dst):
                for i in range(TG):
                    t = TG * g + i
                    ins = nc.tensor.transpose(dst[:, P * i:P * (i + 1)], src[:, t, :], ident[:])
                ins.then_inc(tr[s], 1)

            def warm(n, dst):
                for _ in range(n):
                    mm(dst[:, 0:P], ones[:], ones[:], start=True, stop=True)

            def project0(g):
                pe_.wait_ge(xtr[0], g + 1)
                if g >= 2:
                    pe_.wait_ge(gates, 3 * (g - 1))
                for w in range(3):
                    ins = mm(bank[2 + 3 * (g % 2) + w][:], w_rec[:, w, :], xT[:, G * g:G * (g + 1)], start=True, stop=True)
                ins.then_inc(proj0, 1)

            def turn_back(g, dst):
                pe_.wait_ge(scanned, g + 1)
                for i in range(TG):
                    t = TG * g + i
                    ins = nc.tensor.transpose(dst[:, P * i:P * (i + 1)], hT[:, P * t:P * (t + 1)], ident[:])
                ins.then_inc(back, 1)

            def turn1(g):
                pe_.wait_ge(rms, TG * (g + 1))
                pe_.wait_ge(res1, g + 1)
                turn(1, g, xrms, bank[g % 2])

            def route(b):
                pe_.wait_ge(xtr[1], GB * (b + 1))
                for t in range(TB):
                    tok = T * b + P * t
                    ins = mm(bank[0][:, NE * t:NE * (t + 1)], xT[:, tok:tok + P], wr0_sb[:], start=True, stop=True)
                ins.then_inc(rout, 1)

            pe_.wait_ge(consts, 5)
            warm(24, bank[5])
            pe_.wait_ge(ld_rec, ALL_REC)
            for b in range(B):
                for g in range(GB * b, GB * (b + 1)):
                    pe_.wait_ge(xnr[0], TG * (g + 1))
                    if b:
                        pe_.wait_ge(xtr[0], g - 1)
                    turn(0, g, xn, bank[g % 2])
                for g in range(GB * b, GB * (b + 1)):
                    project0(g)
            pe_.wait_ge(xtr[0], NG)
            turn_back(0, bank[0])
            turn_back(1, bank[1])
            turn_back(2, bank[2])
            turn_back(3, bank[3])
            turn1(0)
            turn1(1)
            pe_.wait_ge(ld_w, ALL_W)
            route(0)

            def expert_down(v):
                w = v // GB
                pe_.wait_ge(hd, HC * (v + 1))
                pe_.wait_ge(ld_down[w % 2], 16 * (w // 2 + 1))
                if v >= 2:
                    pe_.wait_ge(cmb, v - 1)
                for c in range(HC):
                    for i in range(TG):
                        ins = mm(bank[6 + v % 2][:, D * i:D * (i + 1)], hid[:, (HC * v + c) % 4, P * i:P * (i + 1)],
                                 wexp_sb[:, w % 2, 2 * HID + D * c:2 * HID + D * (c + 1)],
                                 start=(c == 0 and i == 0), stop=(c == HC - 1), skip_group_check=True)
                ins.then_inc(dn, 1)

            def expert(w):
                pe_.wait_ge(wsplit, 2 * (w + 1))
                if w % NE == 0:
                    pe_.wait_ge(xrest, GB * (w // NE + 1))
                for v in range(w * GB, (w + 1) * GB):
                    g = w // NE * GB + v % GB
                    for c in range(HC):
                        u = v * HC + c
                        if u >= 2:
                            pe_.wait_ge(hd, u - 1)
                        for r in range(2):
                            f = HID * (1 - r) + P * c
                            dst, tok = bank[2 + 2 * (u % 2) + r][:], slice(G * g, G * (g + 1))
                            rounded, rest = wsp[:, w % 2, 0, f:f + P], wsp[:, w % 2, 1, f:f + P]
                            mm(dst, rounded, xhi[:, tok], start=True, stop=False)
                            mm(dst, rounded, xlo[:, tok], start=False, stop=False)
                            ins = mm(dst, rest, xhi[:, tok], start=False, stop=True)
                        ins.then_inc(up, 1)
                    if v:
                        expert_down(v - 1)

            pe_.wait_ge(gates, 3 * NG)
            pe_.wait_ge(res1, NG)
            for w in range(3):
                expert(w)
            pe_.wait_ge(routed, 1)
            turn1(2)
            turn1(3)
            expert(3)
            route(1)
            for w in range(4, NE + 3):
                expert(w)
                if w == 4:
                    pe_.wait_ge(wsq, 1)
                    pe_.wait_ge(consts, 5)
                    pe_.wait_ge(xtr[1], NG)
                    for c in range(FC):
                        ins = mm(bank[1][:, c:c + 1], wv2[:, P * c:P * (c + 1)], ones[:, 0:1], start=True, stop=True)
                    ins.then_inc(vn, 1)
                elif w == 6:
                    pe_.wait_ge(vdg, 1)
                    for c in range(FC):
                        ins = mm(bank[1][:, P * c:P * (c + 1)], ones[:], wv2[:, P * c:P * (c + 1)], start=True, stop=True)
                    ins.then_inc(vbc, 1)
            pe_.wait_ge(routed, 2)
            pe_.wait_ge(wvr, 1)
            for g in range(GB):
                pe_.wait_ge(xnr[2], TG * (g + 1))
                turn(2, g, xn, bank[g % 2])
            for w in range(NE + 3, 2 * NE):
                expert(w)
            expert_down(2 * NE * GB - 1)

            def values(t, dst):
                mm(dst[:], xT[:, P * t:P * (t + 1)], wv_sb[:], start=True, stop=True).then_inc(vp, 1)

            last = []

            def shared_bank(work, i):
                if last:
                    before, n = last.pop()
                    if before == "project":
                        pe_.wait_ge(qkd, n + 1)
                    elif before == "max_turn":
                        pe_.wait_ge(nm, n + 1)
                    elif before == "turn":
                        pe_.wait_ge(xtr[2], n + 1)
                    elif before == "values":
                        pe_.wait_ge(vr, n + 1)
                    elif before == "out_turn":
                        pe_.wait_ge(otr, n + 1)
                    elif before == "out":
                        pe_.wait_ge(res3, n + 1)
                    elif before == "ffn_turn":
                        pe_.wait_ge(xtr[3], n + 1)
                    elif before == "ffn_scores":
                        pe_.wait_ge(idx, 2 * n + 1)
                    elif before == "ffn_up":
                        pe_.wait_ge(h2r, n + 1)
                    elif before == "ffn_down" and n % TG == TG - 1:
                        pe_.wait_ge(res4, n // TG + 1)
                last.append((work, i))

            def project(pr, r):
                b, col = pr // (NH // 2), P * (r // 2)
                dst = bank[6 if pr else 2 + r]
                if pr:
                    shared_bank("project", 4 * pr + r)
                tok = T * b + G * (r % 2)
                mm(dst[:], wqk_sb[:, pr % (NH // 2), col:col + P], xT[:, tok:tok + G], start=True, stop=True).then_inc(pj, 1)

            def max_chunk(n, m):
                i, c, w = CHUNKS[m]
                u = NC * n + m
                last = c == i // TG
                pr, a = n // 2, n % 2
                own = HALF[a]
                if m == 0:
                    pe_.wait_ge(hi, 4 * (n // 2) + 2 * (n % 2) + 2)
                if u >= 2:
                    pe_.wait_ge(mr, u - 1)
                ins = mm(bank[u % 2][:, 0:w], qs[own, pr % 2, a, P * i:P * (i + 1)],
                         kd[own, pr % 2, a, G * c:G * c + w], start=True, stop=True)
                if last:
                    ins = mm(bank[u % 2][:, w - P:w], identb[:], maskb[:], start=False, stop=True, skip_group_check=True)
                ins.then_inc(mp, 1)

            def max_turn(n):
                pe_.wait_ge(mf, n + 1)
                shared_bank("max_turn", n)
                nc.tensor.transpose(bank[6][0:TB, 0:P], mfin[:, n % 2, :], ident[:]).then_inc(mt, 1)

            def score(n, k):
                g, j, q0, w = STEPS[k]
                u = NS * n + k
                pr, a = n // 2, n % 2
                if k == 0:
                    pe_.wait_ge(mrow, 16 * (n + 1))
                if k == 0 and a == 0:
                    pe_.wait_ge(dup, 64 * (pr + 1))
                    pe_.wait_ge(qlo, 2 * (pr + 1))
                    pe_.wait_ge(klo, 2 * (pr + 1))
                if u >= 3:
                    pe_.wait_ge(ex, u - 2)
                diag = q0 == P * j
                dst = bank[SCORE_BANKS[u % 3]]
                keys, queries, rows = slice(P * j, P * (j + 1)), slice(q0, q0 + w), WITH_SHIFT[a]
                mm(dst[:, 0:w], kd[:, pr % 2, a, keys], qs[:, pr % 2, a, queries], start=True, stop=False)
                ins = mm(dst[:, 0:w], kl[rows, pr % 2, a, keys], qm[rows, pr % 2, a, queries], start=False, stop=True)
                if diag:
                    ins = mm(dst[:, 0:P], identb[:], masktb[:], start=False, stop=True, skip_group_check=True)
                ins.then_inc(st, 1)

            def weigh(n, k):
                g, j, q0, w = STEPS[k]
                u = NS * n + k
                b, h = n // NH, n % NH
                pe_.wait_ge(ex, u + 1)
                by_pool, by_vector = rests(n, k)
                if k in POOL_STEPS:
                    pe_.wait_ge(plp, by_pool)
                else:
                    pe_.wait_ge(pld, by_vector)
                if j == 0 and n:
                    pe_.wait_ge(on, 2 * (n - 1) + g + 1)
                for i in range(w // P):
                    at = (q0 - G * g) // P + i
                    dst = bank[4 + g][:, (HD + 1) * at:(HD + 1) * (at + 1)]
                    rounded, rest = ph[:, u % PT_RING, P * i:P * (i + 1)], pl[:, u % PT_RING, P * i:P * (i + 1)]
                    v = vals[:, TB * b + j, h, :]
                    mm(dst, rounded, v[:, 0:HD + 1], start=(j == 0 and i == 0), stop=False, skip_group_check=True)
                    mm(dst[:, 0:HD], rounded, v[:, VREST:VREST + HD], start=False, stop=False, skip_group_check=True)
                    ins = mm(dst, rest, v[:, 0:HD + 1], start=False, stop=(j == TG * g + at), skip_group_check=True)
                ins.then_inc(pv, 1)

            def out_turn(t, dst):
                for c in range(FC):
                    ins = nc.tensor.transpose(dst[:, P * c:P * (c + 1)], att[:, t, P * c:P * (c + 1)], ident[:])
                ins.then_inc(ot, 1)

            def out_project(t, dst):
                pe_.wait_ge(otr, t + 1)
                pe_.wait_ge(wor, 1)
                for c in range(FC):
                    ins = mm(dst, attT[:, t % 2, c, :], wo_sb[:, c, :], start=(c == 0), stop=(c == FC - 1))
                ins.then_inc(yo, 1)

            def ffn_scores(b):
                pe_.wait_ge(mnr, b + 1)
                mm(bank[6][0:1, 0:NE], mean_sb[:, b:b + 1], wr1_sb[:], start=True, stop=True).then_inc(sc, 1)

            def ffn_up(u, dst):
                g, c = u // FC, u % FC
                b = g // GB
                pe_.wait_ge(ld_ffn[b], 16)
                mm(dst[:], wffn_sb[b][:, P * c:P * (c + 1)], xT[:, G * g:G * (g + 1)], start=True, stop=True).then_inc(h2, 1)

            def ffn_down(t, bank_):
                g, i = t // TG, t % TG
                b = g // GB
                pe_.wait_ge(h2r, FC * (g + 1))
                pe_.wait_ge(ld_ffn2[b], 32)
                dst = bank_[:, D * i:D * (i + 1)]
                for c in range(FC):
                    mm(dst, hid2[:, g % 2, c, P * i:P * (i + 1)], wffn_sb[b][:, FF + FC + D * c:FF + FC + D * (c + 1)],
                       start=(c == 0), stop=False)
                ins = mm(dst, ones[0:1, :], b2_sb[:, b, :], start=False, stop=True)
                if i == TG - 1:
                    ins.then_inc(y2, 1)

            pe_.wait_ge(hd, 2 * NE * GB * HC)
            for r in range(4):
                project(0, r)
            pe_.wait_ge(consts, 5)
            pe_.wait_ge(narrowed, 3)
            pe_.wait_ge(krow, 4)
            pe_.wait_ge(cmb, 2 * NE * GB)
            def beside(work, i):
                shared_bank(work, i)
                if work == "turn":
                    pe_.wait_ge(xnr[2], TG * (i + 1))
                    turn(2, i, xn, bank[6])
                elif work == "values":
                    pe_.wait_ge(xtr[2], NG)
                    values(i, bank[6])
                elif work == "out_turn":
                    pe_.wait_ge(on, 2 * NH)
                    out_turn(i, bank[6])
                elif work == "out":
                    out_project(i, bank[6][:, 0:D])
                elif work == "ffn_turn":
                    pe_.wait_ge(xnr[3], TG * (i + 1))
                    turn(3, i, xn, bank[6])
                elif work == "ffn_scores":
                    ffn_scores(0)
                elif work == "ffn_up":
                    ffn_up(i, bank[6])
                elif work == "ffn_down":
                    ffn_down(i, bank[6])

            for t in range(TB):
                if t < 4:
                    pe_.wait_ge(qkd, t + 1)
                else:
                    pe_.wait_ge(vr, t - 3)
                values(t, bank[2 + t % 4])
                if t >= 3:
                    max_chunk(0, 2 * (t - 3))
                    max_chunk(0, 2 * (t - 3) + 1)
            for m in range(10, NC):
                max_chunk(0, m)
            max_turn(0)
            for m in range(NC - TURN_AT):
                max_chunk(1, m)
            pe_.wait_ge(vr, TB)
            for n in range(NHD):
                pr = n // 2 + 1
                nxt = n % 2 == 0 and pr < NP
                for k in range(NS):
                    score(n, k)
                    for lag in (LAG + 1, LAG) if k % 2 else ():
                        if k >= lag:
                            weigh(n, k - lag)
                        elif n:
                            weigh(n - 1, NS + k - lag)
                    ahead, m = MAX_AT[k]
                    if n + ahead < NHD:
                        max_chunk(n + ahead, m)
                    if nxt and k in PROJ_AT:
                        project(pr, PROJ_AT[k])
                    work, i = BESIDE.get(n, {}).get(k, ("", 0))
                    if work:
                        beside(work, i)
                    if n + 1 < NHD and k == TURN_AT:
                        max_turn(n + 1)
            for k in range(NS - LAG, NS):
                weigh(NHD - 1, k)

            pe_.wait_ge(on, 2 * NHD)
            pe_.wait_ge(ex, NS * NHD)
            out_turn(TB, bank[TB % 2])
            for t in range(TB, NT):
                if t + 1 < NT:
                    if t > TB:
                        pe_.wait_ge(otr, t)
                    out_turn(t + 1, bank[(t + 1) % 2])
                out_project(t, bank[2 + t // TG % 2][:, D * (t % TG):D * (t % TG + 1)])
            pe_.wait_ge(otr, NT)
            warm(24, bank[7])
            for g in range(GB, NG):
                pe_.wait_ge(xnr[3], TG * (g + 1))
                turn(3, g, xn, bank[g % 2])
            pe_.wait_ge(res4, GB)
            ffn_scores(1)
            warm(18, bank[7])
            for g in range(GB, NG):
                for u in range(FC * g, FC * (g + 1)):
                    if u >= FC * GB + 2:
                        pe_.wait_ge(h2r, u - 1)
                    ffn_up(u, bank[4 + u % 2])
            for g in range(GB, NG):
                for t in range(TG * g, TG * (g + 1)):
                    ffn_down(t, bank[2 + g % 2])


def kernel(L0_attn_x, L0_attn_Wg, L0_attn_bg, L0_attn_Wv, L0_attn_bv, L0_attn_Wd, L0_attn_bd, L0_ffn_norm_scale,
           L0_ffn_w_router, L0_ffn_w_up, L0_ffn_w_down, L1_attn_Wqkv, L1_attn_Wo, L1_ffn_Wr, L1_ffn_br, L1_ffn_W1,
           L1_ffn_b1, L1_ffn_W2, L1_ffn_b2):
    import numpy as np
    import concourse.bacc as bacc
    from concourse.bass_utils import run_bass_kernel_spmd

    def arr(a):
        return np.ascontiguousarray(np.asarray(a))

    wqkv = arr(L1_attn_Wqkv).reshape(NH // 2, 2, 3, HD, D)
    wqk = wqkv[:, :, 0:2].transpose(4, 0, 2, 1, 3).reshape(D, NH // 2, 2 * P)
    wv = wqkv[:, :, 2].transpose(3, 0, 1, 2).reshape(D, NH * HD)
    w_up = arr(L0_ffn_w_up).transpose(0, 2, 1)
    w_down = arr(L0_ffn_w_down).reshape(NE, D, HC, P).transpose(0, 3, 2, 1).reshape(NE, P, HC * D)
    w2 = arr(L1_ffn_W2).reshape(NE, FC, P, D).transpose(0, 2, 1, 3).reshape(NE, P, FC * D)
    b1 = arr(L1_ffn_b1).reshape(NE, FC, P).transpose(0, 2, 1)

    pos = np.arange(T, dtype=np.float32)[:, None]
    div = np.exp(np.arange(0, HD, 2, dtype=np.float32) * np.float32(-np.log(10000.0) / HD)).astype(np.float32)
    ang = (pos * div).astype(np.float32)
    table = np.stack([np.sin(ang), np.cos(ang)], axis=-1).reshape(T, HD).astype(np.float32)
    late = np.triu(np.full((P, P), -3.0e38, np.float32), 1)

    arrays = {
        "x": arr(L0_attn_x).reshape(B * T, D), "wg": arr(L0_attn_Wg), "wv0": arr(L0_attn_Wv), "wd": arr(L0_attn_Wd),
        "gate_bias": np.stack([arr(L0_attn_bg), arr(L0_attn_bv), arr(L0_attn_bd)], axis=1),
        "ns": arr(L0_ffn_norm_scale).reshape(D, 1), "wr0": arr(L0_ffn_w_router).T,
        "wexp": np.concatenate([w_up, w_down], axis=2), "wqk": wqk, "wv": wv,
        "wo": arr(L1_attn_Wo).T.reshape(FC, P, D).transpose(1, 0, 2), "wr1": arr(L1_ffn_Wr),
        "br1": arr(L1_ffn_br).reshape(1, NE),
        "wffn": np.concatenate([arr(L1_ffn_W1), b1, w2], axis=2), "b2": arr(L1_ffn_b2),
        "ident_d": np.eye(P, dtype=np.float32), "mask_d": late, "maskt_d": late.T,
        "pe_d": np.concatenate([table.T, table.T], axis=0),
        "iota_d": np.tile(np.arange(NE, dtype=np.float32), (P, 1)),
    }
    arrays = {k: np.ascontiguousarray(v) for k, v in arrays.items()}
    nc = bacc.Bacc("TRN2", target_bir_lowering=False, num_devices=1)
    args = [nc.dram_tensor(k, v.shape, mybir.dt.from_np(v.dtype), kind="ExternalInput").ap() for k, v in arrays.items()]
    args.append(nc.dram_tensor("out", (B * T, D), F32, kind="ExternalOutput").ap())
    mixed_layers_kernel(nc, *args)
    r = run_bass_kernel_spmd(nc, [arrays], core_ids=[0])
    return r.results[0]["out"].reshape(B, T, D)
```
